# Optimizing a Trainium2 kernel written in Bass

```python
import numpy as np
import jax
import jax.numpy as jnp

def _softmax(x, axis=-1):
    return jax.nn.softmax(x, axis=axis)

def _gelu(x):
    return jax.nn.gelu(x, approximate=True)

def _silu(x):
    return jax.nn.silu(x)

def _sigmoid(x):
    return jax.nn.sigmoid(x)

def _layernorm(x, axis=-1, eps=1e-05):
    m = jnp.mean(x, axis=axis, keepdims=True)
    v = jnp.var(x, axis=axis, keepdims=True)
    return (x - m) / jnp.sqrt(v + eps)

def _scatter_add(tgt, idx, src, axis=0):
    return tgt.at[idx].add(src)

def _segment_sum(src, seg, n):
    return jax.ops.segment_sum(src, seg, n)
kernel_name = 'mk_gnn_preln_d2_gnn_r8_002305'

def setup_inputs(seed: int=0):
    np.random.seed(seed)
    _w = jnp.asarray

    def _rec_inputs():
        import jax
        import jax.numpy as jnp
        _gk = jax.random.key(seed)
        x = -0.0005121 + 1.001 * jax.random.normal(jax.random.fold_in(_gk, 1), (12500, 32), jnp.float32)
        src = jax.random.randint(jax.random.fold_in(_gk, 2), (200000,), 0, 12500, jnp.int32)
        dst = jax.random.randint(jax.random.fold_in(_gk, 3), (200000,), 0, 12500, jnp.int32)
        _o = jnp.argsort(dst, stable=True)
        src = src[_o]
        dst = dst[_o]
        edge_attr_32 = 0.000216709 + 1.00012 * jax.random.normal(jax.random.fold_in(_gk, 12), (200000, 32), jnp.float32)
        edge_attr_4 = 0.000714719 + 1.00021 * jax.random.normal(jax.random.fold_in(_gk, 13), (200000, 4), jnp.float32)
        return (x, src, dst, edge_attr_32, edge_attr_4)
    x, src, dst, edge_attr_32, edge_attr_4 = _rec_inputs()

    def _L0_gnn_setup():
        import jax, jax.numpy as jnp
        import numpy as np
        MUL = 8
        N_NODES = 12500
        N_EDGES = 100000
        EDGE_DIM = 32
        MLP_DIM = 64
        W_NUMEL = 4 * MUL * MUL
        ALPHA = 0.25
        C110 = 1.0 / np.sqrt(3.0)
        SI_SCALE = 1.0 / np.sqrt(MUL)
        key = jax.random.key(seed)
        ks = jax.random.split(key, 10)
        node_attr = jax.random.normal(ks[0], (N_NODES, 4 * MUL), dtype=jnp.float32)
        edge_index = jax.random.randint(ks[1], (2, N_EDGES), 0, N_NODES, dtype=jnp.int64)
        edge_sh = jax.random.normal(ks[2], (N_EDGES, 4), dtype=jnp.float32)
        edge_feat = jax.random.normal(ks[3], (N_EDGES, EDGE_DIM), dtype=jnp.float32)
        W1 = jax.random.normal(ks[4], (EDGE_DIM, MLP_DIM), dtype=jnp.float32) / np.sqrt(EDGE_DIM)
        b1 = jnp.zeros((MLP_DIM,), dtype=jnp.float32)
        W2 = jax.random.normal(ks[5], (MLP_DIM, W_NUMEL), dtype=jnp.float32) / np.sqrt(MLP_DIM)
        b2 = jnp.zeros((W_NUMEL,), dtype=jnp.float32)
        si_w0 = jax.random.normal(ks[6], (MUL, MUL), dtype=jnp.float32)
        si_w1 = jax.random.normal(ks[7], (MUL, MUL), dtype=jnp.float32)
        return {'node_attr': node_attr, 'edge_index': edge_index, 'edge_sh': edge_sh, 'edge_feat': edge_feat, 'W1': W1, 'b1': b1, 'W2': W2, 'b2': b2, 'si_w0': si_w0, 'si_w1': si_w1}
    _L0_gnn_all = _L0_gnn_setup()
    _L0_gnn_in = {k: v for k, v in _L0_gnn_all.items() if k in ('W1', 'b1', 'W2', 'b2', 'si_w0', 'si_w1')}
    del _L0_gnn_all

    def _L1_gnn_setup():
        import jax, jax.numpy as jnp
        import numpy as np
        N_NODES = 12500
        N_EDGES = 200000
        D_FEAT = 32
        key = jax.random.key(seed)
        k_feat, k_src, k_dst = jax.random.split(key, 3)
        feat = jax.random.normal(k_feat, (N_NODES, D_FEAT), dtype=jnp.float32)
        eps = jnp.zeros((1,), dtype=jnp.float32)
        edge_src = jax.random.randint(k_src, (N_EDGES,), 0, N_NODES, dtype=jnp.int32)
        edge_dst = jax.random.randint(k_dst, (N_EDGES,), 0, N_NODES, dtype=jnp.int32)
        return {'feat': feat, 'eps': eps, 'edge_src': edge_src, 'edge_dst': edge_dst}
    _L1_gnn_all = _L1_gnn_setup()
    _L1_gnn_in = {k: v for k, v in _L1_gnn_all.items() if k in ('eps',)}
    del _L1_gnn_all
    return {'x': x, 'src': src, 'dst': dst, 'edge_attr_32': edge_attr_32, 'edge_attr_4': edge_attr_4, 'L0_gnn_W1': _L0_gnn_in['W1'], 'L0_gnn_b1': _L0_gnn_in['b1'], 'L0_gnn_W2': _L0_gnn_in['W2'], 'L0_gnn_b2': _L0_gnn_in['b2'], 'L0_gnn_si_w0': _L0_gnn_in['si_w0'], 'L0_gnn_si_w1': _L0_gnn_in['si_w1'], 'L1_gnn_eps': _L1_gnn_in['eps']}

def reference(x, src, dst, edge_attr_32, edge_attr_4, L0_gnn_W1, L0_gnn_b1, L0_gnn_W2, L0_gnn_b2, L0_gnn_si_w0, L0_gnn_si_w1, L1_gnn_eps):
    import jax
    import jax.numpy as jnp

    def _L0_gnn_ref(node_attr, edge_index, edge_sh, edge_feat, W1, b1, W2, b2, si_w0, si_w1):
        import jax, jax.numpy as jnp
        import numpy as np
        MUL = 8
        N_NODES = 12500
        N_EDGES = 100000
        EDGE_DIM = 32
        MLP_DIM = 64
        W_NUMEL = 4 * MUL * MUL
        ALPHA = 0.25
        C110 = 1.0 / np.sqrt(3.0)
        SI_SCALE = 1.0 / np.sqrt(MUL)
        n = node_attr.shape[0]
        e = edge_sh.shape[0]
        h = jax.nn.relu(edge_feat @ W1 + b1)
        w = (h @ W2 + b2).reshape(e, 4, MUL, MUL)
        w_000, w_011, w_101, w_110 = (w[:, 0], w[:, 1], w[:, 2], w[:, 3])
        s = node_attr[:, :MUL]
        v = node_attr[:, MUL:].reshape(n, MUL, 3)
        src, dst = (edge_index[0], edge_index[1])
        s_e = s[src]
        v_e = v[src]
        sh0 = edge_sh[:, 0]
        sh1 = edge_sh[:, 1:4]
        m0 = ALPHA * (jnp.einsum('ei,eio->eo', s_e * sh0[:, None], w_000) + C110 * jnp.einsum('eim,em,eio->eo', v_e, sh1, w_110))
        m1 = ALPHA * (jnp.einsum('ei,em,eio->eom', s_e, sh1, w_011) + jnp.einsum('eim,eio->eom', v_e * sh0[:, None, None], w_101))
        out0 = jax.ops.segment_sum(m0, dst, num_segments=n)
        out1 = jax.ops.segment_sum(m1.reshape(e, MUL * 3), dst, num_segments=n).reshape(n, MUL, 3)
        out0 = out0 + SI_SCALE * (s @ si_w0)
        out1 = out1 + SI_SCALE * jnp.einsum('nim,io->nom', v, si_w1)
        return jnp.concatenate([out0, out1.reshape(n, MUL * 3)], axis=-1)

    def _L1_gnn_ref(feat, eps, edge_src, edge_dst):
        import jax, jax.numpy as jnp
        import numpy as np
        N_NODES = 12500
        N_EDGES = 200000
        D_FEAT = 32
        neigh = jax.ops.segment_sum(feat[edge_src], edge_dst, num_segments=feat.shape[0])
        return (1.0 + eps) * feat + neigh
    edge_index = jnp.stack([src, dst])
    h = jnp.maximum(_layernorm(x, axis=-1), 0.0)
    x = x + _L0_gnn_ref(h, edge_index, edge_attr_4, edge_attr_32, L0_gnn_W1, L0_gnn_b1, L0_gnn_W2, L0_gnn_b2, L0_gnn_si_w0, L0_gnn_si_w1)
    h = jnp.maximum(_layernorm(x, axis=-1), 0.0)
    x = x + _L1_gnn_ref(h, L1_gnn_eps, src, dst)
    return x

_drawn_inputs = setup_inputs


def setup_inputs(seed=0):
    import zlib

    import numpy as np

    out = dict(_drawn_inputs(seed))
    spreads = {'L0_gnn_b1': (0.0, 0.1), 'L0_gnn_b2': (0.0, 0.1)}
    factors = {}
    for name, (base, spread) in spreads.items():
        noise = np.random.default_rng([zlib.crc32(name.encode()), seed]).standard_normal(out[name].shape)
        drawn = base * np.exp(spread * noise) if base else spread * noise
        out[name] = jnp.asarray(drawn.astype(out[name].dtype))
    for name, factor in factors.items():
        out[name] = (out[name] * factor).astype(out[name].dtype)
    return out
```

```python
from contextlib import ExitStack

import numpy as np

import concourse.bass as bass
from concourse import mybir
from concourse.alu_op_type import AluOpType as ALU

F32 = mybir.dt.float32
I32 = mybir.dt.int32
ACT = mybir.ActivationFunctionType
AX = mybir.AxisListType

P = 128
N_NODES, D = 12500, 32
N_EDGES, D_EDGE, D_MLP, MUL = 200000, 32, 64, 8
SLOTS = -(-N_NODES // P)
NODES = SLOTS * P
TILES = 8
GROUP = TILES * P
QUAD = TILES // 2 * P
GROUPS = 2 * -(-N_EDGES // (2 * GROUP))
EDGES = GROUPS * GROUP
PAIRS = GROUPS // 2
WIN = P
W_NUMEL = 4 * MUL * MUL
ALPHA = 0.25
C110 = 1.0 / float(np.sqrt(3.0))
SI_SCALE = 1.0 / float(np.sqrt(MUL))
EPS = 1e-5
CHUNK = 16
CHUNKS = -(-SLOTS // CHUNK)


def build(nc, x, src, dst_groups, dst_tiles, edge_t, sh, w1, b1, w2, b2, si0, si1, eps, out):
    table_1 = nc.dram_tensor("table_1", (NODES, D), F32).ap()
    table_2 = nc.dram_tensor("table_2", (NODES, D), F32).ap()
    group_table = nc.dram_tensor("group_table", (GROUPS * 2,), I32).ap()

    ctx = ExitStack()
    with ctx:
        def sb(name, shape, dt=F32):
            return ctx.enter_context(nc.sbuf_tensor(name, shape, dt))

        def ps(name, shape):
            return ctx.enter_context(nc.psum_tensor(name, shape, F32))

        def sem(name):
            return ctx.enter_context(nc.semaphore(name))

        x_nm = sb("x_nm", [P, SLOTS, D])
        h_nm = sb("h_nm", [P, SLOTS, D])
        scratch = sb("scratch", [P, SLOTS, D])
        stat = sb("stat", [P, 4, SLOTS])
        eps_ln = sb("eps_ln", [P, 1])
        eps_gin = sb("eps_gin", [P, 1])
        one_plus_eps = sb("one_plus_eps", [P, 1])
        iota_i = sb("iota_i", [P, P], I32)
        iota = sb("iota", [P, P])
        identity = sb("identity", [P, P])
        w1_sb = sb("w1_sb", [D_EDGE, D_MLP])
        b1_sb = sb("b1_sb", [D_MLP, 1])
        w2_sb = sb("w2_sb", [D_MLP + 1, W_NUMEL])
        si_sb = sb("si_sb", [P, P])
        h_t = sb("h_t", [P, 2, P])
        dst_g = sb("dst_g", [PAIRS, 2, GROUP], I32)
        lo_hi = sb("lo_hi", [PAIRS, 2, 2])
        base_flag = sb("base_flag", [PAIRS, 2, 2], I32)
        table = sb("table", [P, GROUPS, 2], I32)
        flags = sb("flags", [1, GROUPS])
        ones_row = sb("ones_row", [1, GROUPS])
        far_upto = sb("far_upto", [1, GROUPS])
        past = sb("past", [PAIRS, 2])
        far_rounds = sb("far_rounds", [1, GROUPS], I32)
        dst_i = sb("dst_i", [P, GROUPS * TILES], I32)
        dst_loc = sb("dst_loc", [P, GROUPS * TILES])
        idx = [sb(f"idx{j}", [P, TILES], I32) for j in range(2)]
        z = [sb(f"z{j}", [P, TILES, D]) for j in range(2)]
        sh_sb = [sb(f"sh{j}", [P, TILES, 4]) for j in range(2)]
        edge_sb = [sb(f"edge{j}", [D_EDGE, GROUP]) for j in range(2)]
        hid = [sb(f"hid{q}", [D_MLP + 1, QUAD]) for q in range(2)]
        onehot = [sb(f"onehot{j}", [P, TILES, WIN]) for j in range(2)]
        msg = [sb(f"msg{j}", [P, TILES, D]) for j in range(2)]
        u = sb("u", [P, TILES, 2 * MUL])
        v_sh = sb("v_sh", [P, TILES, MUL, 3])
        prod_a = [sb(f"prod_a{q}", [P, 4, MUL, 2 * MUL]) for q in range(2)]
        prod_bc = [sb(f"prod_bc{q}", [P, 4, 4, MUL, MUL]) for q in range(2)]
        sums = sb("sums", [P, TILES, 4, MUL])
        p_sh = sb("p_sh", [P, TILES, 3, MUL])
        far = sb("far", [P, TILES])
        onehot_far = sb("onehot_far", [P, TILES, WIN])
        rows_of = [slice(k * D, (k + 1) * D) for k in range(2)]
        acc_sb = sb("acc_sb", [2 * D, NODES + WIN])
        acc = [acc_sb[rows_of[k], :] for k in range(2)]

        hid_ps = [ps(f"hid_ps{q}", [P, QUAD]) for q in range(2)]
        w_ps = [ps(f"w_ps{q}", [P, 4, W_NUMEL]) for q in range(2)]
        win_ps = ps("win_ps", [P, 512])[:, 0:WIN]
        far_ps = ps("far_ps", [P, 512])[:, 0:WIN]

        s_x = sem("s_x")
        s_weights = sem("s_weights")
        s_dst = sem("s_dst")
        s_group_out = sem("s_group_out")
        s_group_in = sem("s_group_in")
        s_si = sem("s_si")
        s_iota = sem("s_iota")
        s_iota_f = sem("s_iota_f")
        s_ident = sem("s_ident")
        s_zero = sem("s_zero")
        s_ones = sem("s_ones")
        s_lo_hi = sem("s_lo_hi")
        s_past = sem("s_past")
        s_w2 = sem("s_w2")
        s_inv = sem("s_inv")
        s_flags = sem("s_flags")
        s_eps = sem("s_eps")
        s_base = sem("s_base")
        s_tables = sem("s_tables")
        s_ln = sem("s_ln")
        s_sq = sem("s_sq")
        s_std = sem("s_std")
        s_h = sem("s_h")
        s_table = [sem("s_table1"), sem("s_table2")]
        s_ht = sem("s_ht")
        s_ht_sb = sem("s_ht_sb")
        s_si_mm = sem("s_si_mm")
        s_x1 = sem("s_x1")
        s_nm = [sem("s_nm1"), sem("s_nm2")]
        s_nm_add = [sem("s_nm_add1"), sem("s_nm_add2")]
        s_x3 = sem("s_x3")
        s_out = sem("s_out")
        s_idx = [[sem(f"s_idx{k}{j}") for j in range(2)] for k in range(2)]
        s_z = [[sem(f"s_z{k}{j}") for j in range(2)] for k in range(2)]
        s_sh = [sem(f"s_sh{j}") for j in range(2)]
        s_edge = [sem(f"s_edge{j}") for j in range(2)]
        s_hid_mm = sem("s_hid_mm")
        s_hid = sem("s_hid")
        s_w_mm = sem("s_w_mm")
        s_onehot = [sem(f"s_onehot{k}") for k in range(2)]
        s_vsh = sem("s_vsh")
        s_u = sem("s_u")
        s_prod_bc = sem("s_prod_bc")
        s_prod = sem("s_prod")
        s_sum_bc = sem("s_sum_bc")
        s_sum_a = sem("s_sum_a")
        s_q = sem("s_q")
        s_msg = sem("s_msg")
        s_win = [sem(f"s_win{k}") for k in range(2)]
        s_acc = [sem(f"s_acc{k}") for k in range(2)]
        s_started = sem("s_started")
        s_far_done = sem("s_far_done")
        s_far_dst = [sem(f"s_far_dst{k}") for k in range(2)]
        s_far_onehot = [sem(f"s_far_onehot{k}") for k in range(2)]
        s_far_win = [sem(f"s_far_win{k}") for k in range(2)]
        s_far_acc = [sem(f"s_far_acc{k}") for k in range(2)]

        block = ctx.enter_context(nc.Block())

        @block.sync
        def _(sp):
            sp.dma_start(x_nm[:, :, :], x).then_inc(s_x, 16)
            sp.dma_start(eps_gin[:, :], eps.to_broadcast([P, 1])).then_inc(s_weights, 16)
            sp.dma_start(w1_sb[:, :], w1).then_inc(s_weights, 16)
            sp.dma_start(b1_sb[:, :], b1).then_inc(s_weights, 16)
            sp.dma_start(w2_sb[0:D_MLP, :], w2).then_inc(s_weights, 16)
            sp.dma_start(w2_sb[D_MLP:D_MLP + 1, :], b2).then_inc(s_weights, 16)
            sp.dma_start(dst_g[:, :, :], dst_groups).then_inc(s_dst, 16)
            sp.dma_start(dst_i[:, :], dst_tiles).then_inc(s_dst, 16)
            sp.wait_ge(s_zero, 1)
            for b in range(P // MUL):
                sp.dma_start(si_sb[b * MUL:(b + 1) * MUL, b * MUL:(b + 1) * MUL],
                             si0 if b % 4 == 0 else si1).then_inc(s_si, 16)

            def loads(g, i, j, first):
                if not first:
                    sp.wait_ge(s_z[0][j], 16 * TILES * i)
                sp.dma_start(idx[j][:, :], src[g, :, :]).then_inc(s_idx[0][j], 16)
                if not first:
                    sp.wait_ge(s_hid_mm, 2 * g - 2)
                sp.dma_start(edge_sb[j][:, :], edge_t[g, :, :]).then_inc(s_edge[j], 16)
                if not first:
                    sp.wait_ge(s_msg, g - 1)
                sp.dma_start(sh_sb[j][:, :, :], sh[g, :, :, :]).then_inc(s_sh[j], 16)

            for j in range(2):
                loads(j, 0, j, True)
            sp.wait_ge(s_h, 1)
            sp.dma_start(table_1.rearrange("(p s) d -> p s d", s=SLOTS), h_nm[:, :, :])\
              .then_inc(s_table[0], 16)
            sp.wait_ge(s_base, 2)
            sp.dma_start(group_table.rearrange("(p n) -> p n", n=4),
                         base_flag[:, :, :].rearrange("p a b -> p (a b)")).then_inc(s_group_out, 16)
            sp.wait_ge(s_group_out, 16)
            sp.dma_start(table[:, :, :].rearrange("p a b -> p (a b)"),
                         group_table.partition_broadcast(P)).then_inc(s_group_in, 16)
            with sp.Fori(1, PAIRS) as i:
                for j in range(2):
                    loads(2 * i + j, i, j, False)
            for j in range(2):
                sp.wait_ge(s_z[0][j], 16 * TILES * PAIRS)
                sp.dma_start(idx[j][:, :], src[j, :, :]).then_inc(s_idx[1][j], 16)
            sp.wait_ge(s_h, 2)
            sp.dma_start(table_2.rearrange("(p s) d -> p s d", s=SLOTS), h_nm[:, :, :])\
              .then_inc(s_table[1], 16)
            with sp.Fori(1, PAIRS) as i:
                for j in range(2):
                    sp.wait_ge(s_z[1][j], 16 * TILES * i)
                    sp.dma_start(idx[j][:, :], src[2 * i + j, :, :]).then_inc(s_idx[1][j], 16)
            for c in range(CHUNKS):
                a, b = c * CHUNK, min((c + 1) * CHUNK, SLOTS)
                sp.wait_ge(s_nm_add[1], c + 1)
                sp.dma_start(out[:, a:b, :], x_nm[:, a:b, :]).then_inc(s_out, 16)
            sp.wait_ge(s_out, 16 * CHUNKS)

        @block.gpsimd
        def _(pool):
            pool.iota(iota_i[:, :], pattern=[[1, P]], base=0, channel_multiplier=0).then_inc(s_iota, 1)
            pool.memset(identity[:, :], 0.0).then_inc(s_ident, 1)
            pool.memset(si_sb[:, :], 0.0).then_inc(s_zero, 1)
            pool.wait_ge(s_ident, 1)
            pool.affine_select(out=identity[:, :], in_=identity[:, :], compare_op=ALU.not_equal,
                               fill=1.0, base=0, pattern=[[-1, P]], channel_multiplier=1)\
                .then_inc(s_ident, 1)
            pool.memset(acc_sb[:, :], 0.0).then_inc(s_zero, 1)

            def gather(k, table_dram, i, j):
                pool.wait_ge(s_idx[k][j], 16 * (i + 1))
                pool.sem_inc(s_started, 1)
                for t in range(TILES):
                    pool.indirect_dma_start(
                        out=z[j][:, t, :], out_offset=None, in_=table_dram,
                        in_offset=bass.IndirectOffsetOnAxis(ap=idx[j][:, t:t + 1], axis=0),
                    ).then_inc(s_z[k][j], 16)

            pool.wait_ge(s_table[0], 16)
            for j in range(2):
                gather(0, table_1, 0, j)
            with pool.Fori(1, PAIRS) as i:
                for j in range(2):
                    pool.wait_ge(s_prod, 2 * (2 * i + j) - 2)
                    gather(0, table_1, i, j)
            pool.wait_ge(s_table[1], 16)
            for j in range(2):
                gather(1, table_2, 0, j)
            with pool.Fori(1, PAIRS) as i:
                for j in range(2):
                    pool.wait_ge(s_win[1], 2 * i + j - 1)
                    gather(1, table_2, i, j)

        @block.scalar
        def _(act):
            def norm(k):
                act.wait_ge(s_ln, 3 * k + 2)
                act.activation(scratch[:, :, :], h_nm[:, :, :], ACT.Square).then_inc(s_sq, 1)
                act.wait_ge(s_ln, 3 * k + 3)
                act.wait_ge(s_eps, 1)
                act.activation(stat[:, 2, :], stat[:, 1, :], ACT.Sqrt, bias=eps_ln[:, :],
                               scale=1.0 / D).then_inc(s_std, 1)

            norm(0)
            for n in range(-(-SLOTS // 4)):
                rows = min(4, SLOTS - 4 * n) * D
                act.wait_ge(s_ht, n + 1)
                if n >= 2:
                    act.wait_ge(s_si_mm, n - 1)
                act.activation(h_t[0:rows, n % 2, :], hid_ps[n % 2][0:rows, 0:P], ACT.Copy,
                               scale=SI_SCALE).then_inc(s_ht_sb, 1)
            act.wait_ge(s_weights, 80)
            act.wait_ge(s_ones, 2)

            def hidden(g, first):
                for q in range(2):
                    act.wait_ge(s_hid_mm, 2 * g + q + 1)
                    if not first:
                        act.wait_ge(s_w_mm, 2 * g + q - 1)
                    act.activation(hid[q][0:D_MLP, :], hid_ps[q][0:D_MLP, :], ACT.Relu,
                                   bias=b1_sb[:, :]).then_inc(s_hid, 1)

            hidden(0, True)
            hidden(1, False)
            with act.Fori(1, PAIRS) as i:
                for j in range(2):
                    hidden(2 * i + j, False)
            norm(1)

        @block.tensor
        def _(pe):
            def scatter(k, gg, j, rows):
                flag = pe.value_load(table[0:1, gg, 1:2], min_val=0, max_val=1)
                with pe.If(flag):
                    done = pe.value_load(far_rounds[0:1, bass.ds(gg, 1)], min_val=0, max_val=GROUPS * SLOTS)
                    with pe.Fori(0, SLOTS) as w:
                        pe.wait_ge(s_far_onehot[k], done + w + 1)
                        pe.wait_ge(s_far_acc[k], done + w + 1)
                        for t in range(TILES):
                            mm = pe.matmul(far_ps[rows_of[k], :], rows[:, t, :], onehot_far[:, t, :],
                                           start=(t == 0), stop=(t == TILES - 1))
                        mm.then_inc(s_far_win[k], 1)
                if not (isinstance(gg, int) and gg == 0):
                    pe.wait_ge(s_acc[k], gg)
                for t in range(TILES):
                    mm = pe.matmul(win_ps[rows_of[k], :], rows[:, t, :], onehot[j][:, t, :],
                                   start=(t == 0), stop=(t == TILES - 1))
                mm.then_inc(s_win[k], 1)

            def to_node_major(k):
                for c in range(CHUNKS):
                    if c >= 2:
                        pe.wait_ge(s_nm_add[k], c - 1)
                    nm = w_ps[c % 2][:, 0:2, :].rearrange("p a (s d) -> p (a s) d", d=D)
                    for s in range(c * CHUNK, min((c + 1) * CHUNK, SLOTS)):
                        mm = pe.matmul(nm[:, s % CHUNK, :], acc[k][:, s:NODES:SLOTS],
                                       identity[rows_of[k], rows_of[k]], start=True, stop=True)
                    mm.then_inc(s_nm[k], 1)

            pe.wait_ge(s_ident, 2)
            pe.wait_ge(s_h, 1)
            pe.wait_ge(s_si, 16 * (P // MUL))
            n_fours = -(-SLOTS // 4)

            def self_product(n):
                rows = min(4, SLOTS - 4 * n) * D
                c = n // 4
                nm = w_ps[c % 2][:, 0:2, :].rearrange("p a d -> p (a d)")
                pe.wait_ge(s_ht_sb, n + 1)
                if n % 4 == 0 and c >= 2:
                    pe.wait_ge(s_x1, c - 1)
                pe.matmul(nm[:, (n % 4) * P:(n % 4) * P + rows], h_t[0:rows, n % 2, :],
                          si_sb[0:rows, 0:rows], start=True, stop=True).then_inc(s_si_mm, 1)

            for n in range(n_fours):
                rows = min(4, SLOTS - 4 * n) * D
                if n >= 2:
                    pe.wait_ge(s_ht_sb, n - 1)
                pe.transpose(hid_ps[n % 2][0:rows, 0:P],
                             h_nm[:, 4 * n:4 * n + rows // D, :].rearrange("p s d -> p (s d)"),
                             identity[:, :]).then_inc(s_ht, 1)
                if n >= 1:
                    self_product(n - 1)
            self_product(n_fours - 1)
            pe.wait_ge(s_w2, 3)
            pe.wait_ge(s_weights, 80)

            def weights(g, i, j, first):
                pe.wait_ge(s_edge[j], 16 * (i + 1))
                for q in range(2):
                    if first:
                        pe.wait_ge(s_ht_sb, n_fours)
                    else:
                        pe.wait_ge(s_hid, 2 * g + q - 1)
                    pe.matmul(hid_ps[q][0:D_MLP, :], w1_sb[:, :],
                              edge_sb[j][:, q * QUAD:(q + 1) * QUAD],
                              start=True, stop=True).then_inc(s_hid_mm, 1)
                for q in range(2):
                    pe.wait_ge(s_hid, 2 * g + q + 1)
                    if first:
                        pe.wait_ge(s_x1, CHUNKS)
                    else:
                        pe.wait_ge(s_prod, 2 * g + q - 1)
                    for t in range(4):
                        mm = pe.matmul(w_ps[q][:, t, :], hid[q][:, t * P:(t + 1) * P], w2_sb[:, :],
                                       start=True, stop=True)
                    mm.then_inc(s_w_mm, 1)

            pe.wait_ge(s_tables, 2)
            weights(0, 0, 0, True)
            weights(1, 0, 1, False)
            pe.wait_ge(s_msg, 1)
            scatter(0, 0, 0, msg[0])
            with pe.Fori(1, PAIRS) as i:
                for j in range(2):
                    g = 2 * i + j
                    weights(g, i, j, False)
                    pe.wait_ge(s_msg, g)
                    scatter(0, g - 1, 1 - j, msg[1 - j])
            pe.wait_ge(s_msg, GROUPS)
            scatter(0, GROUPS - 1, 1, msg[1])
            pe.wait_ge(s_acc[0], GROUPS)
            to_node_major(0)

            def neighbours(g, i, j):
                pe.wait_ge(s_z[1][j], 16 * TILES * (i + 1))
                pe.wait_ge(s_onehot[1], g + 1)
                scatter(1, g, j, z[j])

            for j in range(2):
                neighbours(j, 0, j)
            with pe.Fori(1, PAIRS) as i:
                for j in range(2):
                    neighbours(2 * i + j, i, j)
            pe.wait_ge(s_acc[1], GROUPS)
            to_node_major(1)

        @block.vector
        def _(dve):
            def norm(k):
                dve.tensor_reduce(stat[:, 0, :], x_nm[:, :, :], AX.X, ALU.add).then_inc(s_ln, 1)
                dve.wait_ge(s_ln, 3 * k + 1)
                dve.scalar_tensor_tensor(
                    out=h_nm[:, :, :], in0=stat[:, 0, :].unsqueeze(2).broadcast_to([P, SLOTS, D]),
                    scalar=-1.0 / D, in1=x_nm[:, :, :], op0=ALU.mult, op1=ALU.add).then_inc(s_ln, 1)
                dve.wait_ge(s_sq, k + 1)
                dve.tensor_reduce(stat[:, 1, :], scratch[:, :, :], AX.X, ALU.add).then_inc(s_ln, 1)
                dve.wait_ge(s_std, k + 1)
                dve.reciprocal(stat[:, 3, :], stat[:, 2, :]).then_inc(s_inv, 1)
                dve.wait_ge(s_inv, k + 1)
                dve.scalar_tensor_tensor(
                    out=h_nm[:, :, :], in0=h_nm[:, :, :], scalar=0.0,
                    in1=stat[:, 3, :].unsqueeze(2).broadcast_to([P, SLOTS, D]),
                    op0=ALU.max, op1=ALU.mult).then_inc(s_h, 1)

            for k in range(2):
                dve.sem_inc(s_far_acc[k], 1)
                dve.sem_inc(s_far_win[k], 1)
            dve.memset(eps_ln[:, :], EPS).then_inc(s_eps, 1)
            dve.memset(ones_row[:, :], 1.0).then_inc(s_eps, 1)
            for q in range(2):
                dve.memset(hid[q][D_MLP:D_MLP + 1, :], 1.0).then_inc(s_ones, 1)
            dve.wait_ge(s_x, 16)
            norm(0)
            dve.wait_ge(s_dst, 32)
            dve.tensor_reduce(lo_hi[:, :, 0], dst_g[:, :, :], AX.X, ALU.min).then_inc(s_lo_hi, 1)
            dve.tensor_reduce(lo_hi[:, :, 1], dst_g[:, :, :], AX.X, ALU.max).then_inc(s_lo_hi, 1)
            dve.wait_ge(s_lo_hi, 2)
            dve.scalar_tensor_tensor(out=past[:, :], in0=lo_hi[:, :, 1], scalar=float(-WIN),
                                     in1=lo_hi[:, :, 0], op0=ALU.add, op1=ALU.subtract)\
               .then_inc(s_past, 1)
            dve.tensor_copy(base_flag[:, :, 0], lo_hi[:, :, 0]).then_inc(s_base, 1)
            dve.wait_ge(s_past, 1)
            dve.tensor_scalar(base_flag[:, :, 1], past[:, :], 0.0, None, ALU.is_ge).then_inc(s_base, 1)
            dve.wait_ge(s_weights, 80)
            part_a = w2_sb[:, 0:2 * MUL * MUL].rearrange("k (o i) -> k o i", i=2 * MUL)
            dve.tensor_scalar(part_a[:, :, MUL:], part_a[:, :, MUL:], ALPHA * C110, None, ALU.mult)\
               .then_inc(s_w2, 1)
            dve.tensor_scalar(part_a[:, :, 0:MUL], part_a[:, :, 0:MUL], ALPHA, None, ALU.mult)\
               .then_inc(s_w2, 1)
            dve.tensor_scalar(w2_sb[:, 2 * MUL * MUL:], w2_sb[:, 2 * MUL * MUL:], ALPHA, None, ALU.mult)\
               .then_inc(s_w2, 1)
            dve.tensor_scalar(one_plus_eps[:, :], eps_gin[:, :], 1.0, None, ALU.add).then_inc(s_eps, 1)
            dve.wait_ge(s_iota, 1)
            dve.tensor_copy(iota[:, :], iota_i[:, :]).then_inc(s_iota_f, 1)
            dve.wait_ge(s_group_in, 16)
            dve.tensor_tensor(dst_loc[:, :].rearrange("p (g t) -> p g t", t=TILES),
                              dst_i[:, :].rearrange("p (g t) -> p g t", t=TILES),
                              table[:, :, 0:1].broadcast_to([P, GROUPS, TILES]), ALU.subtract)\
               .then_inc(s_tables, 1)
            dve.tensor_scalar(flags[:, :], table[0:1, :, 1], float(SLOTS), None, ALU.mult)\
               .then_inc(s_flags, 1)
            dve.wait_ge(s_flags, 1)
            dve.wait_ge(s_eps, 2)
            dve.tensor_tensor_scan(far_upto[:, :], ones_row[:, :], flags[:, :], 0.0, ALU.mult, ALU.add)\
               .then_inc(s_flags, 1)
            dve.wait_ge(s_flags, 2)
            dve.tensor_tensor(far_rounds[:, :], far_upto[:, :], flags[:, :], ALU.subtract)\
               .then_inc(s_tables, 1)
            for c in range(CHUNKS):
                a, b = c * CHUNK, min((c + 1) * CHUNK, SLOTS)
                dve.wait_ge(s_si_mm, min(4 * (c + 1), -(-SLOTS // 4)))
                nm = w_ps[c % 2][:, 0:2, :].rearrange("p a (s d) -> p (a s) d", d=D)
                dve.tensor_tensor(x_nm[:, a:b, :], x_nm[:, a:b, :], nm[:, 0:b - a, :], ALU.add)\
                   .then_inc(s_x1, 1)
            dve.wait_ge(s_tables, 2)
            dve.wait_ge(s_iota_f, 1)
            dve.wait_ge(s_zero, 2)

            def one_hot(k, g, j):
                dve.tensor_tensor(
                    onehot[j][:, :, :], iota[:, :].unsqueeze(1).broadcast_to([P, TILES, WIN]),
                    dst_loc[:, bass.ds(g * TILES, TILES)].unsqueeze(2).broadcast_to([P, TILES, WIN]),
                    ALU.is_equal).then_inc(s_onehot[k], 1)

            def accumulate(k, gg, j, first):
                if not first:
                    dve.wait_ge(s_acc[k], gg)
                flag = dve.value_load(table[0:1, gg, 1:2], min_val=0, max_val=1)
                with dve.If(flag):
                    done = dve.value_load(far_rounds[0:1, bass.ds(gg, 1)], min_val=0, max_val=GROUPS * SLOTS)
                    at = bass.ds(gg * TILES, TILES)
                    dve.tensor_scalar(far[:, :], dst_loc[:, at], float(WIN), None, ALU.is_ge)\
                       .then_inc(s_far_dst[k], 1)
                    dve.drain()
                    dve.scalar_tensor_tensor(out=far[:, :], in0=dst_i[:, at], scalar=1.0,
                                             in1=far[:, :], op0=ALU.add, op1=ALU.mult)
                    dve.drain()
                    dve.tensor_scalar(far[:, :], far[:, :], -1.0, None, ALU.add)
                    with dve.Fori(0, SLOTS) as w:
                        dve.drain()
                        dve.wait_ge(s_far_win[k], done + w + 1)
                        dve.tensor_tensor(
                            onehot_far[:, :, :], iota[:, :].unsqueeze(1).broadcast_to([P, TILES, WIN]),
                            far[:, :].unsqueeze(2).broadcast_to([P, TILES, WIN]),
                            ALU.is_equal).then_inc(s_far_onehot[k], 1)
                        dve.drain()
                        dve.tensor_scalar(far[:, :], far[:, :], float(-WIN), None, ALU.add)
                        dve.wait_ge(s_far_win[k], done + w + 2)
                        window = acc[k][:, bass.ds(w * WIN, WIN)]
                        dve.tensor_tensor(window, window, far_ps[rows_of[k], :], ALU.add)\
                           .then_inc(s_far_acc[k], 1)
                    dve.wait_ge(s_far_acc[k], done + SLOTS + 1)
                    dve.sem_inc(s_far_done, 1)
                dve.wait_ge(s_win[k], gg + 1)
                base = dve.value_load(table[0:1, gg, 0:1], min_val=0, max_val=NODES - 1)
                window = acc[k][:, bass.ds(base, WIN)]
                dve.tensor_tensor(window, window, win_ps[rows_of[k], :], ALU.add).then_inc(s_acc[k], 1)

            def messages(g, i, j, first):
                m, zz, s = msg[j], z[j], sh_sb[j]
                if not isinstance(g, int):
                    dve.wait_ge(s_win[0], g - 1)
                one_hot(0, g, j)
                dve.wait_ge(s_z[0][j], 16 * TILES * (i + 1))
                dve.wait_ge(s_sh[j], 16 * (i + 1))
                if not first:
                    dve.wait_ge(s_u, 2 * g)
                    dve.wait_ge(s_prod, 2 * g)
                dve.tensor_tensor(
                    v_sh[:, :, :, :].rearrange("p t i m -> p t m i"),
                    zz[:, :, MUL:].rearrange("p t (m i) -> p t m i", m=3),
                    s[:, :, 1:4].unsqueeze(3).broadcast_to([P, TILES, 3, MUL]), ALU.mult)\
                   .then_inc(s_vsh, 1)
                dve.tensor_tensor(u[:, :, 0:MUL], zz[:, :, 0:MUL],
                                  s[:, :, 0:1].broadcast_to([P, TILES, MUL]), ALU.mult)\
                   .then_inc(s_u, 1)
                dve.wait_ge(s_vsh, g + 1)
                dve.tensor_reduce(u[:, :, MUL:], v_sh[:, :, :, :], AX.X, ALU.add).then_inc(s_u, 1)
                for q in range(2):
                    ts = slice(4 * q, 4 * q + 4)
                    w = w_ps[q]
                    dve.wait_ge(s_w_mm, 2 * g + q + 1)
                    if not first:
                        dve.wait_ge(s_sum_bc, 2 * g + q - 1)
                    dve.tensor_tensor(
                        prod_bc[q][:, :, 0, :, :],
                        w[:, :, 128:192].rearrange("p t (o i) -> p t o i", i=MUL),
                        zz[:, ts, 0:MUL].unsqueeze(2).broadcast_to([P, 4, MUL, MUL]), ALU.mult)\
                       .then_inc(s_prod_bc, 1)
                    for c in range(3):
                        dve.tensor_tensor(
                            prod_bc[q][:, :, 1 + c, :, :],
                            w[:, :, 192:256].rearrange("p t (o i) -> p t o i", i=MUL),
                            zz[:, ts, MUL * (1 + c):MUL * (2 + c)].unsqueeze(2)
                            .broadcast_to([P, 4, MUL, MUL]), ALU.mult).then_inc(s_prod_bc, 1)
                    dve.wait_ge(s_u, 2 * g + 2)
                    if not first:
                        dve.wait_ge(s_sum_a, 2 * g + q - 1)
                    dve.tensor_tensor(
                        prod_a[q][:, :, :, :],
                        w[:, :, 0:128].rearrange("p t (o i) -> p t o i", i=2 * MUL),
                        u[:, ts, :].unsqueeze(2).broadcast_to([P, 4, MUL, 2 * MUL]), ALU.mult)\
                       .then_inc(s_prod, 1)
                if not first:
                    dve.wait_ge(s_q, 2 * g)
                for q in range(2):
                    ts = slice(4 * q, 4 * q + 4)
                    dve.wait_ge(s_prod_bc, 8 * g + 4 * q + 4)
                    dve.tensor_reduce(sums[:, ts, :, :].rearrange("p t c o -> p (t c o)"),
                                      prod_bc[q][:, :, :, :, :].rearrange("p t c o i -> p (t c o) i"),
                                      AX.X, ALU.add).then_inc(s_sum_bc, 1)
                    dve.wait_ge(s_prod, 2 * g + q + 1)
                    dve.tensor_reduce(m[:, ts, 0:MUL], prod_a[q][:, :, :, :], AX.X, ALU.add)\
                       .then_inc(s_sum_a, 1)
                dve.wait_ge(s_sum_bc, 2 * g + 2)
                dve.tensor_tensor(
                    m[:, :, MUL:].rearrange("p t (m o) -> p t m o", m=3), sums[:, :, 1:4, :],
                    s[:, :, 0:1].unsqueeze(3).broadcast_to([P, TILES, 3, MUL]), ALU.mult)\
                   .then_inc(s_q, 1)
                if not first:
                    dve.wait_ge(s_msg, g)
                dve.tensor_tensor(
                    p_sh[:, :, :, :], sums[:, :, 0:1, :].broadcast_to([P, TILES, 3, MUL]),
                    s[:, :, 1:4].unsqueeze(3).broadcast_to([P, TILES, 3, MUL]), ALU.mult)\
                   .then_inc(s_q, 1)
                dve.wait_ge(s_q, 2 * g + 2)
                dve.wait_ge(s_sum_a, 2 * g + 2)
                dve.tensor_tensor(
                    m[:, :, MUL:], m[:, :, MUL:], p_sh[:, :, :, :].rearrange("p t m o -> p t (m o)"),
                    ALU.add).then_inc(s_msg, 1)

            messages(0, 0, 0, True)
            messages(1, 0, 1, False)
            accumulate(0, 0, 0, True)
            with dve.Fori(1, PAIRS) as i:
                for j in range(2):
                    g = 2 * i + j
                    messages(g, i, j, False)
                    accumulate(0, g - 1, 1 - j, False)
            accumulate(0, GROUPS - 1, 1, False)

            def add_chunks(k):
                for c in range(CHUNKS):
                    a, b = c * CHUNK, min((c + 1) * CHUNK, SLOTS)
                    dve.wait_ge(s_nm[k], c + 1)
                    nm = w_ps[c % 2][:, 0:2, :].rearrange("p a (s d) -> p (a s) d", d=D)
                    dve.tensor_tensor(x_nm[:, a:b, :], x_nm[:, a:b, :], nm[:, 0:b - a, :], ALU.add)\
                       .then_inc(s_nm_add[k], 1)

            add_chunks(0)
            dve.wait_ge(s_nm_add[0], CHUNKS)
            norm(1)
            dve.wait_ge(s_h, 2)
            dve.wait_ge(s_eps, 3)
            dve.scalar_tensor_tensor(out=x_nm[:, :, :], in0=h_nm[:, :, :], scalar=one_plus_eps[:, :],
                                     in1=x_nm[:, :, :], op0=ALU.mult, op1=ALU.add).then_inc(s_x3, 1)

            one_hot(1, 0, 0)
            one_hot(1, 1, 1)
            accumulate(1, 0, 0, True)
            with dve.Fori(1, PAIRS) as i:
                for j in range(2):
                    g = 2 * i + j
                    dve.wait_ge(s_win[1], g - 1)
                    one_hot(1, g, j)
                    accumulate(1, g - 1, 1 - j, False)
            accumulate(1, GROUPS - 1, 1, False)
            dve.wait_ge(s_x3, 1)
            add_chunks(1)


FEATURES = np.concatenate([np.arange(MUL), MUL + np.arange(3 * MUL).reshape(MUL, 3).T.ravel()])


def weight_order():
    cols = np.arange(W_NUMEL).reshape(4, MUL, MUL)
    w_000, w_011, w_101, w_110 = (c.T for c in cols)
    return np.concatenate([np.concatenate([w_000, w_110], axis=1).ravel(), w_011.ravel(), w_101.ravel()])


def kernel(x, src, dst, edge_attr_32, edge_attr_4, L0_gnn_W1, L0_gnn_b1, L0_gnn_W2, L0_gnn_b2,
           L0_gnn_si_w0, L0_gnn_si_w1, L1_gnn_eps):
    import concourse.bacc as bacc
    from concourse.bass_utils import run_bass_kernel_spmd

    def padded(a, n, value=0):
        a = np.asarray(a)
        out = np.full((n,) + a.shape[1:], value, a.dtype)
        out[:a.shape[0]] = a
        return out

    order = weight_order()
    dst_p = padded(dst, EDGES, NODES - 1)
    arrays = {
        "x": padded(x, NODES)[:, FEATURES].reshape(P, SLOTS, D),
        "src": padded(src, EDGES).reshape(GROUPS, P, TILES),
        "dst_groups": dst_p.reshape(PAIRS, 2, GROUP),
        "dst_tiles": dst_p.reshape(GROUPS, P, TILES).transpose(1, 0, 2).reshape(P, GROUPS * TILES),
        "edge_t": padded(edge_attr_32, EDGES).reshape(GROUPS, P, TILES, D_EDGE)
        .transpose(0, 3, 2, 1).reshape(GROUPS, D_EDGE, GROUP),
        "sh": padded(edge_attr_4, EDGES).reshape(GROUPS, P, TILES, 4),
        "w1": np.asarray(L0_gnn_W1),
        "b1": np.asarray(L0_gnn_b1).reshape(D_MLP, 1),
        "w2": np.asarray(L0_gnn_W2)[:, order],
        "b2": np.asarray(L0_gnn_b2)[order].reshape(1, W_NUMEL),
        "si0": np.asarray(L0_gnn_si_w0),
        "si1": np.asarray(L0_gnn_si_w1),
        "eps": np.asarray(L1_gnn_eps).reshape(1, 1),
    }
    nc = bacc.Bacc("TRN2", target_bir_lowering=False, num_devices=1)
    args, ins = [], {}
    for name, a in arrays.items():
        a = np.ascontiguousarray(a)
        ins[f"in_{name}"] = a
        args.append(nc.dram_tensor(f"in_{name}", a.shape, mybir.dt.from_np(a.dtype),
                                   kind="ExternalInput").ap())
    args.append(nc.dram_tensor("out_nodes", (P, SLOTS, D), F32, kind="ExternalOutput").ap())
    build(nc, *args)
    r = run_bass_kernel_spmd(nc, [ins], core_ids=[0])
    got = r.results[0]["out_nodes"].reshape(NODES, D)[:N_NODES]
    back = np.empty(D, np.int64)
    back[FEATURES] = np.arange(D)
    return np.ascontiguousarray(got[:, back])
```

```python
from contextlib import ExitStack

import numpy as np

import concourse.bass as bass
from concourse import mybir
from concourse.alu_op_type import AluOpType as ALU

F32 = mybir.dt.float32
I32 = mybir.dt.int32
ACT = mybir.ActivationFunctionType
AX = mybir.AxisListType

P = 128
N_NODES, D = 12500, 32
N_EDGES, D_EDGE, D_MLP, MUL = 200000, 32, 64, 8
SLOTS = -(-N_NODES // P)
NODES = SLOTS * P
TILES = 8
GROUP = TILES * P
QUAD = TILES // 2 * P
SUBS = P // D_EDGE
SUB = GROUP // SUBS
GROUPS = 2 * -(-N_EDGES // (2 * GROUP))
EDGES = GROUPS * GROUP
PAIRS = GROUPS // 2
WIN = P
W_NUMEL = 4 * MUL * MUL
ALPHA = 0.25
C110 = 1.0 / float(np.sqrt(3.0))
SI_SCALE = 1.0 / float(np.sqrt(MUL))
EPS = 1e-5
CHUNK = 16
CHUNKS = -(-SLOTS // CHUNK)


def build(nc, x, src, dst_groups, dst_tiles, edge_t, sh, w1, b1, w2, b2, si0, si1, eps, out):
    table_1 = nc.dram_tensor("table_1", (NODES, D), F32).ap()
    table_2 = nc.dram_tensor("table_2", (NODES, D), F32).ap()
    group_table = nc.dram_tensor("group_table", (GROUPS * 2,), I32).ap()

    ctx = ExitStack()
    with ctx:
        def sb(name, shape, dt=F32):
            return ctx.enter_context(nc.sbuf_tensor(name, shape, dt))

        def ps(name, shape):
            return ctx.enter_context(nc.psum_tensor(name, shape, F32))

        def sem(name):
            return ctx.enter_context(nc.semaphore(name))

        x_nm = sb("x_nm", [P, SLOTS, D])
        h_nm = sb("h_nm", [P, SLOTS, D])
        scratch = sb("scratch", [P, SLOTS, D])
        stat = sb("stat", [P, 4, SLOTS])
        eps_ln = sb("eps_ln", [P, 1])
        eps_gin = sb("eps_gin", [P, 1])
        one_plus_eps = sb("one_plus_eps", [P, 1])
        iota_i = sb("iota_i", [P, P], I32)
        neg_iota = sb("neg_iota", [P, P])
        identity = sb("identity", [P, P])
        w1_sb = sb("w1_sb", [P, SUBS, D_MLP])
        b1_sb = sb("b1_sb", [D_MLP, 1])
        w2_sb = sb("w2_sb", [P, W_NUMEL])
        si_sb = sb("si_sb", [P, P])
        h_t = sb("h_t", [P, 2, P])
        dst_g = sb("dst_g", [PAIRS, 2, GROUP], I32)
        lo_hi = sb("lo_hi", [PAIRS, 2, 2])
        base_flag = sb("base_flag", [PAIRS, 2, 2], I32)
        table = sb("table", [P, GROUPS, 2], I32)
        flags = sb("flags", [1, GROUPS])
        ones_row = sb("ones_row", [1, GROUPS])
        far_upto = sb("far_upto", [1, GROUPS])
        past = sb("past", [PAIRS, 2])
        far_rounds = sb("far_rounds", [1, GROUPS], I32)
        dst_i = sb("dst_i", [P, GROUPS * TILES], I32)
        neg_loc = sb("neg_loc", [P, GROUPS * TILES])
        idx = [sb(f"idx{j}", [P, TILES], I32) for j in range(2)]
        z = [sb(f"z{j}", [P, TILES, D]) for j in range(2)]
        sh_sb = [sb(f"sh{j}", [P, TILES, 4]) for j in range(2)]
        edge_sb = [sb(f"edge{j}", [P, SUB]) for j in range(2)]
        hid = [sb(f"hid{q}", [P, QUAD]) for q in range(2)]
        onehot = [sb(f"onehot{j}", [P, TILES, WIN]) for j in range(2)]
        msg = [sb(f"msg{j}", [P, TILES, D]) for j in range(2)]
        distance = sb("distance", [P, TILES, WIN])
        zs = sb("zs", [P, TILES, D + MUL])
        v_sh = sb("v_sh", [P, TILES, MUL, 3])
        prod_a = [sb(f"prod_a{q}", [P, 4, MUL, 2 * MUL]) for q in range(2)]
        prod_bc = [sb(f"prod_bc{q}", [P, 4, 4, MUL, MUL]) for q in range(2)]
        sums = sb("sums", [P, TILES, 4, MUL])
        p_sh = sb("p_sh", [P, TILES, 3, MUL])
        far = sb("far", [P, TILES])
        onehot_far = sb("onehot_far", [P, TILES, WIN])
        rows_of = [slice(k * D, (k + 1) * D) for k in range(2)]
        acc_sb = sb("acc_sb", [2 * D, NODES + WIN])
        acc = [acc_sb[rows_of[k], :] for k in range(2)]

        hid_ps = [ps(f"hid_ps{q}", [P, QUAD]) for q in range(2)]
        w_ps = [ps(f"w_ps{q}", [P, 4, W_NUMEL]) for q in range(2)]
        win_ps = ps("win_ps", [P, 512])[:, 0:WIN]
        far_ps = ps("far_ps", [P, 512])[:, 0:WIN]

        s_x = sem("s_x")
        s_weights = sem("s_weights")
        s_dst = sem("s_dst")
        s_group_out = sem("s_group_out")
        s_group_in = sem("s_group_in")
        s_si = sem("s_si")
        s_iota = sem("s_iota")
        s_iota_f = sem("s_iota_f")
        s_ident = sem("s_ident")
        s_zero = sem("s_zero")
        s_ones = sem("s_ones")
        s_lo_hi = sem("s_lo_hi")
        s_past = sem("s_past")
        s_w2 = sem("s_w2")
        s_inv = sem("s_inv")
        s_flags = sem("s_flags")
        s_eps = sem("s_eps")
        s_base = sem("s_base")
        s_tables = sem("s_tables")
        s_ln = sem("s_ln")
        s_sq = sem("s_sq")
        s_std = sem("s_std")
        s_h = sem("s_h")
        s_table = [sem("s_table1"), sem("s_table2")]
        s_ht = sem("s_ht")
        s_ht_sb = sem("s_ht_sb")
        s_si_mm = sem("s_si_mm")
        s_x1 = sem("s_x1")
        s_nm = [sem("s_nm1"), sem("s_nm2")]
        s_nm_add = [sem("s_nm_add1"), sem("s_nm_add2")]
        s_x3 = sem("s_x3")
        s_out = sem("s_out")
        s_idx = [[sem(f"s_idx{k}{j}") for j in range(2)] for k in range(2)]
        s_z = [[sem(f"s_z{k}{j}") for j in range(2)] for k in range(2)]
        s_sh = [sem(f"s_sh{j}") for j in range(2)]
        s_edge = [sem(f"s_edge{j}") for j in range(2)]
        s_hid_mm = sem("s_hid_mm")
        s_hid = sem("s_hid")
        s_w_mm = sem("s_w_mm")
        s_onehot = [sem(f"s_onehot{k}") for k in range(2)]
        s_vsh = sem("s_vsh")
        s_zs = sem("s_zs")
        s_distance = sem("s_distance")
        s_hid_rows = sem("s_hid_rows")
        s_prod_bc = sem("s_prod_bc")
        s_prod = sem("s_prod")
        s_sum_bc = sem("s_sum_bc")
        s_sum_a = sem("s_sum_a")
        s_p_sh = sem("s_p_sh")
        s_msg = sem("s_msg")
        s_win = [sem(f"s_win{k}") for k in range(2)]
        s_acc = [sem(f"s_acc{k}") for k in range(2)]
        s_started = sem("s_started")
        s_far_done = sem("s_far_done")
        s_far_dst = [sem(f"s_far_dst{k}") for k in range(2)]
        s_far_onehot = [sem(f"s_far_onehot{k}") for k in range(2)]
        s_far_win = [sem(f"s_far_win{k}") for k in range(2)]
        s_far_acc = [sem(f"s_far_acc{k}") for k in range(2)]

        block = ctx.enter_context(nc.Block())

        @block.sync
        def _(sp):
            sp.dma_start(x_nm[:, :, :], x).then_inc(s_x, 16)
            sp.dma_start(eps_gin[:, :], eps.to_broadcast([P, 1])).then_inc(s_weights, 16)
            sp.dma_start(b1_sb[:, :], b1).then_inc(s_weights, 16)
            sp.dma_start(dst_g[:, :, :], dst_groups).then_inc(s_dst, 16)
            sp.dma_start(dst_i[:, :], dst_tiles).then_inc(s_dst, 16)
            sp.wait_ge(s_zero, 3)
            for b in range(P // MUL):
                sp.dma_start(si_sb[b * MUL:(b + 1) * MUL, b * MUL:(b + 1) * MUL],
                             si0 if b % 4 == 3 else si1).then_inc(s_si, 16)

            for b in range(SUBS):
                sp.dma_start(w1_sb[b * D_EDGE:(b + 1) * D_EDGE, b, :], w1).then_inc(s_weights, 16)
            sp.dma_start(w2_sb[0:D_MLP, :], w2).then_inc(s_weights, 16)
            sp.dma_start(w2_sb[D_MLP:D_MLP + 1, :], b2).then_inc(s_weights, 16)

            def loads(g, i, j, first):
                if not first:
                    sp.wait_ge(s_z[0][j], 16 * TILES * i)
                sp.dma_start(idx[j][:, :], src[g, :, :]).then_inc(s_idx[0][j], 16)
                if not first:
                    sp.wait_ge(s_hid_mm, 2 * g - 2)
                sp.dma_start(edge_sb[j][:, :], edge_t[g, :, :]).then_inc(s_edge[j], 16)
                if not first:
                    sp.wait_ge(s_msg, g - 1)
                sp.dma_start(sh_sb[j][:, :, :], sh[g, :, :, :]).then_inc(s_sh[j], 16)

            for j in range(2):
                loads(j, 0, j, True)
            sp.wait_ge(s_h, 1)
            sp.dma_start(table_1.rearrange("(p s) d -> p s d", s=SLOTS), h_nm[:, :, :])\
              .then_inc(s_table[0], 16)
            sp.wait_ge(s_base, 2)
            sp.dma_start(group_table.rearrange("(p n) -> p n", n=4),
                         base_flag[:, :, :].rearrange("p a b -> p (a b)")).then_inc(s_group_out, 16)
            sp.wait_ge(s_group_out, 16)
            sp.dma_start(table[:, :, :].rearrange("p a b -> p (a b)"),
                         group_table.partition_broadcast(P)).then_inc(s_group_in, 16)
            with sp.Fori(1, PAIRS) as i:
                for j in range(2):
                    loads(2 * i + j, i, j, False)
            for j in range(2):
                sp.wait_ge(s_z[0][j], 16 * TILES * PAIRS)
                sp.dma_start(idx[j][:, :], src[j, :, :]).then_inc(s_idx[1][j], 16)
            sp.wait_ge(s_h, 2)
            sp.dma_start(table_2.rearrange("(p s) d -> p s d", s=SLOTS), h_nm[:, :, :])\
              .then_inc(s_table[1], 16)
            with sp.Fori(1, PAIRS) as i:
                for j in range(2):
                    sp.wait_ge(s_z[1][j], 16 * TILES * i)
                    sp.dma_start(idx[j][:, :], src[2 * i + j, :, :]).then_inc(s_idx[1][j], 16)
            for c in range(CHUNKS):
                a, b = c * CHUNK, min((c + 1) * CHUNK, SLOTS)
                sp.wait_ge(s_nm_add[1], c + 1)
                sp.dma_start(out[:, a:b, :], x_nm[:, a:b, :]).then_inc(s_out, 16)
            sp.wait_ge(s_out, 16 * CHUNKS)

        @block.gpsimd
        def _(pool):
            pool.iota(iota_i[:, :], pattern=[[1, P]], base=0, channel_multiplier=0).then_inc(s_iota, 1)
            pool.memset(identity[:, :], 0.0).then_inc(s_ident, 1)
            pool.memset(si_sb[:, :], 0.0).then_inc(s_zero, 1)
            pool.memset(w1_sb[:, :, :], 0.0).then_inc(s_zero, 1)
            pool.memset(w2_sb[:, :], 0.0).then_inc(s_zero, 1)
            pool.wait_ge(s_ident, 1)
            pool.affine_select(out=identity[:, :], in_=identity[:, :], compare_op=ALU.not_equal,
                               fill=1.0, base=0, pattern=[[-1, P]], channel_multiplier=1)\
                .then_inc(s_ident, 1)
            pool.memset(acc_sb[:, :], 0.0).then_inc(s_zero, 1)

            def gather(k, table_dram, i, j):
                pool.wait_ge(s_idx[k][j], 16 * (i + 1))
                pool.sem_inc(s_started, 1)
                for t in range(TILES):
                    pool.indirect_dma_start(
                        out=z[j][:, t, :], out_offset=None, in_=table_dram,
                        in_offset=bass.IndirectOffsetOnAxis(ap=idx[j][:, t:t + 1], axis=0),
                    ).then_inc(s_z[k][j], 16)

            pool.wait_ge(s_table[0], 16)
            for j in range(2):
                gather(0, table_1, 0, j)
            with pool.Fori(1, PAIRS) as i:
                for j in range(2):
                    pool.wait_ge(s_prod, 2 * (2 * i + j) - 2)
                    gather(0, table_1, i, j)
            pool.wait_ge(s_table[1], 16)
            for j in range(2):
                gather(1, table_2, 0, j)
            with pool.Fori(1, PAIRS) as i:
                for j in range(2):
                    pool.wait_ge(s_win[1], 2 * i + j - 1)
                    gather(1, table_2, i, j)

        @block.scalar
        def _(act):
            def norm(k):
                act.wait_ge(s_ln, 3 * k + 2)
                act.activation(scratch[:, :, :], h_nm[:, :, :], ACT.Square).then_inc(s_sq, 1)
                act.wait_ge(s_ln, 3 * k + 3)
                act.wait_ge(s_eps, 1)
                act.activation(stat[:, 2, :], stat[:, 1, :], ACT.Sqrt, bias=eps_ln[:, :],
                               scale=1.0 / D).then_inc(s_std, 1)

            norm(0)
            for n in range(-(-SLOTS // 4)):
                rows = min(4, SLOTS - 4 * n) * D
                act.wait_ge(s_ht, n + 1)
                if n >= 2:
                    act.wait_ge(s_si_mm, n - 1)
                act.activation(h_t[0:rows, n % 2, :], hid_ps[n % 2][0:rows, 0:P], ACT.Copy,
                               scale=SI_SCALE).then_inc(s_ht_sb, 1)
            act.wait_ge(s_weights, 16 * (SUBS + 4))
            act.wait_ge(s_ones, 2)

            def hidden(g, first):
                for q in range(2):
                    act.wait_ge(s_hid_mm, 2 * g + q + 1)
                    if not first:
                        act.wait_ge(s_w_mm, 2 * g + q - 1)
                    act.activation(hid[q][0:D_MLP, :], hid_ps[q][0:D_MLP, :], ACT.Relu,
                                   bias=b1_sb[:, :]).then_inc(s_hid, 1)

            def one_hot(g, j):
                if not (isinstance(g, int) and g == 0):
                    act.wait_ge(s_onehot[0], g)
                for t in range(TILES):
                    act.activation(distance[:, t, :], neg_iota[:, :], ACT.Abs, scale=-1.0,
                                   bias=neg_loc[:, bass.ds(g * TILES + t, 1)]).then_inc(s_distance, 1)
                if not isinstance(g, int):
                    act.wait_ge(s_win[0], g - 1)
                act.wait_ge(s_distance, TILES * (g + 1))
                act.activation(onehot[j][:, :, :], distance[:, :, :], ACT.Relu, bias=1.0,
                               scale=-1.0).then_inc(s_onehot[0], 1)

            hidden(0, True)
            act.wait_ge(s_tables, 2)
            act.wait_ge(s_iota_f, 1)
            one_hot(0, 0)
            hidden(1, False)
            one_hot(1, 1)
            with act.Fori(1, PAIRS) as i:
                for j in range(2):
                    hidden(2 * i + j, False)
                    one_hot(2 * i + j, j)
            norm(1)

        @block.tensor
        def _(pe):
            def scatter(k, gg, j, rows):
                flag = pe.value_load(table[0:1, gg, 1:2], min_val=0, max_val=1)
                with pe.If(flag):
                    done = pe.value_load(far_rounds[0:1, bass.ds(gg, 1)], min_val=0, max_val=GROUPS * SLOTS)
                    with pe.Fori(0, SLOTS) as w:
                        pe.wait_ge(s_far_onehot[k], done + w + 1)
                        pe.wait_ge(s_far_acc[k], done + w + 1)
                        for t in range(TILES):
                            mm = pe.matmul(far_ps[rows_of[k], :], rows[:, t, :], onehot_far[:, t, :],
                                           start=(t == 0), stop=(t == TILES - 1))
                        mm.then_inc(s_far_win[k], 1)
                if not (isinstance(gg, int) and gg == 0):
                    pe.wait_ge(s_acc[k], gg)
                for t in range(TILES):
                    mm = pe.matmul(win_ps[rows_of[k], :], rows[:, t, :], onehot[j][:, t, :],
                                   start=(t == 0), stop=(t == TILES - 1))
                mm.then_inc(s_win[k], 1)

            def to_node_major(k):
                for c in range(CHUNKS):
                    if c >= 2:
                        pe.wait_ge(s_nm_add[k], c - 1)
                    nm = w_ps[c % 2][:, 0:2, :].rearrange("p a (s d) -> p (a s) d", d=D)
                    for s in range(c * CHUNK, min((c + 1) * CHUNK, SLOTS)):
                        mm = pe.matmul(nm[:, s % CHUNK, :], acc[k][:, s:NODES:SLOTS],
                                       identity[rows_of[k], rows_of[k]], start=True, stop=True)
                    mm.then_inc(s_nm[k], 1)

            pe.wait_ge(s_ident, 2)
            pe.wait_ge(s_h, 1)
            pe.wait_ge(s_si, 16 * (P // MUL))
            n_fours = -(-SLOTS // 4)

            def self_product(n):
                rows = min(4, SLOTS - 4 * n) * D
                c = n // 4
                nm = w_ps[c % 2][:, 0:2, :].rearrange("p a d -> p (a d)")
                pe.wait_ge(s_ht_sb, n + 1)
                if n % 4 == 0 and c >= 2:
                    pe.wait_ge(s_x1, c - 1)
                pe.matmul(nm[:, (n % 4) * P:(n % 4) * P + rows], h_t[0:rows, n % 2, :],
                          si_sb[0:rows, 0:rows], start=True, stop=True).then_inc(s_si_mm, 1)

            for n in range(n_fours):
                rows = min(4, SLOTS - 4 * n) * D
                if n >= 2:
                    pe.wait_ge(s_ht_sb, n - 1)
                pe.transpose(hid_ps[n % 2][0:rows, 0:P],
                             h_nm[:, 4 * n:4 * n + rows // D, :].rearrange("p s d -> p (s d)"),
                             identity[:, :]).then_inc(s_ht, 1)
                if n >= 1:
                    self_product(n - 1)
            self_product(n_fours - 1)
            pe.wait_ge(s_w2, 3)
            pe.wait_ge(s_weights, 16 * (SUBS + 4))

            def hidden(g, i, j, first):
                pe.wait_ge(s_edge[j], 16 * (i + 1))
                for q in range(2):
                    if first:
                        pe.wait_ge(s_ht_sb, n_fours)
                    else:
                        pe.wait_ge(s_hid, 2 * g + q - 1)
                    for b in range(2):
                        mm = pe.matmul(hid_ps[q][0:D_MLP, b * SUB:(b + 1) * SUB],
                                       w1_sb[:, 2 * q + b, :], edge_sb[j][:, :], start=True, stop=True)
                    mm.then_inc(s_hid_mm, 1)

            def weights(g, first):
                for q in range(2):
                    pe.wait_ge(s_hid, 2 * g + q + 1)
                    if first:
                        pe.wait_ge(s_x1, CHUNKS)
                    else:
                        pe.wait_ge(s_prod, 2 * g + q - 1)
                    for t in range(4):
                        mm = pe.matmul(w_ps[q][:, t, :], hid[q][:, t * P:(t + 1) * P], w2_sb[:, :],
                                       start=True, stop=True)
                    mm.then_inc(s_w_mm, 1)

            def trip(i):
                for j in range(2):
                    g = 2 * i + j
                    weights(g, isinstance(i, int) and g == 0)
                    if not (isinstance(i, int) and g == GROUPS - 1):
                        hidden(g + 1, i + j, 1 - j, False)
                    if not (isinstance(i, int) and g == 0):
                        pe.wait_ge(s_msg, g)
                        pe.wait_ge(s_onehot[0], g)
                        scatter(0, g - 1, 1 - j, msg[1 - j])

            pe.wait_ge(s_tables, 2)
            hidden(0, 0, 0, True)
            trip(0)
            with pe.Fori(1, PAIRS - 1) as i:
                trip(i)
            trip(PAIRS - 1)
            pe.wait_ge(s_msg, GROUPS)
            pe.wait_ge(s_onehot[0], GROUPS)
            scatter(0, GROUPS - 1, 1, msg[1])
            pe.wait_ge(s_acc[0], GROUPS)
            to_node_major(0)

            def neighbours(g, i, j):
                pe.wait_ge(s_z[1][j], 16 * TILES * (i + 1))
                pe.wait_ge(s_onehot[1], g + 1)
                scatter(1, g, j, z[j])

            for j in range(2):
                neighbours(j, 0, j)
            with pe.Fori(1, PAIRS) as i:
                for j in range(2):
                    neighbours(2 * i + j, i, j)
            pe.wait_ge(s_acc[1], GROUPS)
            to_node_major(1)

        @block.vector
        def _(dve):
            def norm(k):
                dve.tensor_reduce(stat[:, 0, :], x_nm[:, :, :], AX.X, ALU.add).then_inc(s_ln, 1)
                dve.wait_ge(s_ln, 3 * k + 1)
                dve.scalar_tensor_tensor(
                    out=h_nm[:, :, :], in0=stat[:, 0, :].unsqueeze(2).broadcast_to([P, SLOTS, D]),
                    scalar=-1.0 / D, in1=x_nm[:, :, :], op0=ALU.mult, op1=ALU.add).then_inc(s_ln, 1)
                dve.wait_ge(s_sq, k + 1)
                dve.tensor_reduce(stat[:, 1, :], scratch[:, :, :], AX.X, ALU.add).then_inc(s_ln, 1)
                dve.wait_ge(s_std, k + 1)
                dve.reciprocal(stat[:, 3, :], stat[:, 2, :]).then_inc(s_inv, 1)
                dve.wait_ge(s_inv, k + 1)
                dve.scalar_tensor_tensor(
                    out=h_nm[:, :, :], in0=h_nm[:, :, :], scalar=0.0,
                    in1=stat[:, 3, :].unsqueeze(2).broadcast_to([P, SLOTS, D]),
                    op0=ALU.max, op1=ALU.mult).then_inc(s_h, 1)

            for k in range(2):
                dve.sem_inc(s_far_acc[k], 1)
                dve.sem_inc(s_far_win[k], 1)
            dve.memset(eps_ln[:, :], EPS).then_inc(s_eps, 1)
            dve.memset(ones_row[:, :], 1.0).then_inc(s_eps, 1)
            for q in range(2):
                dve.memset(hid[q][D_MLP:, :], 0.0).then_inc(s_hid_rows, 1)
            dve.wait_ge(s_hid_rows, 2)
            for q in range(2):
                dve.memset(hid[q][D_MLP:D_MLP + 1, :], 1.0).then_inc(s_ones, 1)
            dve.wait_ge(s_x, 16)
            norm(0)
            dve.wait_ge(s_dst, 32)
            dve.tensor_reduce(lo_hi[:, :, 0], dst_g[:, :, :], AX.X, ALU.min).then_inc(s_lo_hi, 1)
            dve.tensor_reduce(lo_hi[:, :, 1], dst_g[:, :, :], AX.X, ALU.max).then_inc(s_lo_hi, 1)
            dve.wait_ge(s_lo_hi, 2)
            dve.scalar_tensor_tensor(out=past[:, :], in0=lo_hi[:, :, 1], scalar=float(-WIN),
                                     in1=lo_hi[:, :, 0], op0=ALU.add, op1=ALU.subtract)\
               .then_inc(s_past, 1)
            dve.tensor_copy(base_flag[:, :, 0], lo_hi[:, :, 0]).then_inc(s_base, 1)
            dve.wait_ge(s_past, 1)
            dve.tensor_scalar(base_flag[:, :, 1], past[:, :], 0.0, None, ALU.is_ge).then_inc(s_base, 1)
            dve.wait_ge(s_weights, 16 * (SUBS + 4))
            part_a = w2_sb[:, 0:2 * MUL * MUL].rearrange("k (o i) -> k o i", i=2 * MUL)
            dve.tensor_scalar(part_a[:, :, MUL:], part_a[:, :, MUL:], ALPHA * C110, None, ALU.mult)\
               .then_inc(s_w2, 1)
            dve.tensor_scalar(part_a[:, :, 0:MUL], part_a[:, :, 0:MUL], ALPHA, None, ALU.mult)\
               .then_inc(s_w2, 1)
            dve.tensor_scalar(w2_sb[:, 2 * MUL * MUL:], w2_sb[:, 2 * MUL * MUL:], ALPHA, None, ALU.mult)\
               .then_inc(s_w2, 1)
            dve.tensor_scalar(one_plus_eps[:, :], eps_gin[:, :], 1.0, None, ALU.add).then_inc(s_eps, 1)
            dve.wait_ge(s_iota, 1)
            dve.tensor_scalar(neg_iota[:, :], iota_i[:, :], -1.0, None, ALU.mult).then_inc(s_iota_f, 1)
            dve.wait_ge(s_group_in, 16)
            dve.tensor_tensor(neg_loc[:, :].rearrange("p (g t) -> p g t", t=TILES),
                              table[:, :, 0:1].broadcast_to([P, GROUPS, TILES]),
                              dst_i[:, :].rearrange("p (g t) -> p g t", t=TILES), ALU.subtract)\
               .then_inc(s_tables, 1)
            dve.tensor_scalar(flags[:, :], table[0:1, :, 1], float(SLOTS), None, ALU.mult)\
               .then_inc(s_flags, 1)
            dve.wait_ge(s_flags, 1)
            dve.wait_ge(s_eps, 2)
            dve.tensor_tensor_scan(far_upto[:, :], ones_row[:, :], flags[:, :], 0.0, ALU.mult, ALU.add)\
               .then_inc(s_flags, 1)
            dve.wait_ge(s_flags, 2)
            dve.tensor_tensor(far_rounds[:, :], far_upto[:, :], flags[:, :], ALU.subtract)\
               .then_inc(s_tables, 1)
            for c in range(CHUNKS):
                a, b = c * CHUNK, min((c + 1) * CHUNK, SLOTS)
                dve.wait_ge(s_si_mm, min(4 * (c + 1), -(-SLOTS // 4)))
                nm = w_ps[c % 2][:, 0:2, :].rearrange("p a (s d) -> p (a s) d", d=D)
                dve.tensor_tensor(x_nm[:, a:b, :], x_nm[:, a:b, :], nm[:, 0:b - a, :], ALU.add)\
                   .then_inc(s_x1, 1)
            dve.wait_ge(s_tables, 2)
            dve.wait_ge(s_iota_f, 1)
            dve.wait_ge(s_zero, 4)

            def one_hot(g, j):
                dve.tensor_tensor(
                    onehot[j][:, :, :], neg_iota[:, :].unsqueeze(1).broadcast_to([P, TILES, WIN]),
                    neg_loc[:, bass.ds(g * TILES, TILES)].unsqueeze(2).broadcast_to([P, TILES, WIN]),
                    ALU.is_equal).then_inc(s_onehot[1], 1)

            def accumulate(k, gg, j, first):
                if not first:
                    dve.wait_ge(s_acc[k], gg)
                flag = dve.value_load(table[0:1, gg, 1:2], min_val=0, max_val=1)
                with dve.If(flag):
                    done = dve.value_load(far_rounds[0:1, bass.ds(gg, 1)], min_val=0, max_val=GROUPS * SLOTS)
                    at = bass.ds(gg * TILES, TILES)
                    dve.tensor_scalar(far[:, :], neg_loc[:, at], float(-WIN), None, ALU.is_le)\
                       .then_inc(s_far_dst[k], 1)
                    dve.drain()
                    dve.scalar_tensor_tensor(out=far[:, :], in0=dst_i[:, at], scalar=1.0,
                                             in1=far[:, :], op0=ALU.add, op1=ALU.mult)
                    dve.drain()
                    dve.tensor_scalar(far[:, :], far[:, :], -1.0, 1.0, ALU.mult, ALU.add)
                    with dve.Fori(0, SLOTS) as w:
                        dve.drain()
                        dve.wait_ge(s_far_win[k], done + w + 1)
                        dve.tensor_tensor(
                            onehot_far[:, :, :], neg_iota[:, :].unsqueeze(1).broadcast_to([P, TILES, WIN]),
                            far[:, :].unsqueeze(2).broadcast_to([P, TILES, WIN]),
                            ALU.is_equal).then_inc(s_far_onehot[k], 1)
                        dve.drain()
                        dve.tensor_scalar(far[:, :], far[:, :], float(WIN), None, ALU.add)
                        dve.wait_ge(s_far_win[k], done + w + 2)
                        window = acc[k][:, bass.ds(w * WIN, WIN)]
                        dve.tensor_tensor(window, window, far_ps[rows_of[k], :], ALU.add)\
                           .then_inc(s_far_acc[k], 1)
                    dve.wait_ge(s_far_acc[k], done + SLOTS + 1)
                    dve.sem_inc(s_far_done, 1)
                base = dve.value_load(table[0:1, gg, 0:1], min_val=0, max_val=NODES - 1)

                def add():
                    dve.wait_ge(s_win[k], gg + 1)
                    window = acc[k][:, bass.ds(base, WIN)]
                    dve.tensor_tensor(window, window, win_ps[rows_of[k], :], ALU.add)\
                       .then_inc(s_acc[k], 1)

                return add

            def messages(g, i, j, first):
                out_m, zz, s = msg[j], z[j], sh_sb[j]
                dve.wait_ge(s_z[0][j], 16 * TILES * (i + 1))
                dve.wait_ge(s_sh[j], 16 * (i + 1))
                if not first:
                    dve.wait_ge(s_zs, 2 * g)
                    dve.wait_ge(s_prod, 2 * g)
                dve.tensor_tensor(
                    v_sh[:, :, :, :].rearrange("p t i m -> p t m i"),
                    zz[:, :, 0:3 * MUL].rearrange("p t (m i) -> p t m i", m=3),
                    s[:, :, 1:4].unsqueeze(3).broadcast_to([P, TILES, 3, MUL]), ALU.mult)\
                   .then_inc(s_vsh, 1)
                dve.tensor_tensor(zs[:, :, 0:D], zz[:, :, :],
                                  s[:, :, 0:1].broadcast_to([P, TILES, D]), ALU.mult)\
                   .then_inc(s_zs, 1)
                dve.wait_ge(s_vsh, g + 1)
                dve.tensor_reduce(zs[:, :, D:], v_sh[:, :, :, :], AX.X, ALU.add).then_inc(s_zs, 1)
                for q in range(2):
                    ts = slice(4 * q, 4 * q + 4)
                    w = w_ps[q]
                    dve.wait_ge(s_w_mm, 2 * g + q + 1)
                    if not first:
                        dve.wait_ge(s_sum_bc, 2 * g + q - 1)
                    dve.tensor_tensor(
                        prod_bc[q][:, :, 3, :, :],
                        w[:, :, 128:192].rearrange("p t (o i) -> p t o i", i=MUL),
                        zz[:, ts, 3 * MUL:].unsqueeze(2).broadcast_to([P, 4, MUL, MUL]), ALU.mult)\
                       .then_inc(s_prod_bc, 1)
                    dve.wait_ge(s_zs, 2 * g + 2)
                    for m in range(3):
                        dve.tensor_tensor(
                            prod_bc[q][:, :, m, :, :],
                            w[:, :, 192:256].rearrange("p t (o i) -> p t o i", i=MUL),
                            zs[:, ts, MUL * m:MUL * (m + 1)].unsqueeze(2)
                            .broadcast_to([P, 4, MUL, MUL]), ALU.mult).then_inc(s_prod_bc, 1)
                    if not first:
                        dve.wait_ge(s_sum_a, 2 * g + q - 1)
                    dve.tensor_tensor(
                        prod_a[q][:, :, :, :],
                        w[:, :, 0:128].rearrange("p t (o i) -> p t o i", i=2 * MUL),
                        zs[:, ts, 3 * MUL:].unsqueeze(2).broadcast_to([P, 4, MUL, 2 * MUL]), ALU.mult)\
                       .then_inc(s_prod, 1)
                if not first:
                    dve.wait_ge(s_p_sh, g)
                    dve.wait_ge(s_msg, g)
                if not isinstance(g, int):
                    dve.wait_ge(s_win[0], g - 1)
                for q in range(2):
                    ts = slice(4 * q, 4 * q + 4)
                    dve.wait_ge(s_prod_bc, 8 * g + 4 * q + 4)
                    dve.tensor_reduce(sums[:, ts, :, :].rearrange("p t c o -> p (t c o)"),
                                      prod_bc[q][:, :, :, :, :].rearrange("p t c o i -> p (t c o) i"),
                                      AX.X, ALU.add).then_inc(s_sum_bc, 1)
                    dve.wait_ge(s_prod, 2 * g + q + 1)
                    dve.tensor_reduce(out_m[:, ts, 3 * MUL:], prod_a[q][:, :, :, :], AX.X, ALU.add)\
                       .then_inc(s_sum_a, 1)
                add = None if isinstance(g, int) and g == 0 else \
                    accumulate(0, g - 1, 1 - j, isinstance(g, int) and g == 1)
                dve.wait_ge(s_sum_bc, 2 * g + 2)
                dve.tensor_tensor(
                    p_sh[:, :, :, :], sums[:, :, 3:4, :].broadcast_to([P, TILES, 3, MUL]),
                    s[:, :, 1:4].unsqueeze(3).broadcast_to([P, TILES, 3, MUL]), ALU.mult)\
                   .then_inc(s_p_sh, 1)
                if add is not None:
                    add()
                dve.wait_ge(s_p_sh, g + 1)
                dve.wait_ge(s_sum_a, 2 * g + 2)
                dve.tensor_tensor(
                    out_m[:, :, 0:3 * MUL].rearrange("p t (m o) -> p t m o", m=3),
                    sums[:, :, 0:3, :], p_sh[:, :, :, :], ALU.add).then_inc(s_msg, 1)

            messages(0, 0, 0, True)
            messages(1, 0, 1, False)
            with dve.Fori(1, PAIRS) as i:
                for j in range(2):
                    messages(2 * i + j, i, j, False)
            accumulate(0, GROUPS - 1, 1, False)()

            def add_chunks(k):
                for c in range(CHUNKS):
                    a, b = c * CHUNK, min((c + 1) * CHUNK, SLOTS)
                    dve.wait_ge(s_nm[k], c + 1)
                    nm = w_ps[c % 2][:, 0:2, :].rearrange("p a (s d) -> p (a s) d", d=D)
                    dve.tensor_tensor(x_nm[:, a:b, :], x_nm[:, a:b, :], nm[:, 0:b - a, :], ALU.add)\
                       .then_inc(s_nm_add[k], 1)

            add_chunks(0)
            dve.wait_ge(s_nm_add[0], CHUNKS)
            norm(1)
            dve.wait_ge(s_h, 2)
            dve.wait_ge(s_eps, 3)
            dve.scalar_tensor_tensor(out=x_nm[:, :, :], in0=h_nm[:, :, :], scalar=one_plus_eps[:, :],
                                     in1=x_nm[:, :, :], op0=ALU.mult, op1=ALU.add).then_inc(s_x3, 1)

            one_hot(0, 0)
            one_hot(1, 1)
            accumulate(1, 0, 0, True)()
            with dve.Fori(1, PAIRS) as i:
                for j in range(2):
                    g = 2 * i + j
                    dve.wait_ge(s_win[1], g - 1)
                    one_hot(g, j)
                    accumulate(1, g - 1, 1 - j, False)()
            accumulate(1, GROUPS - 1, 1, False)()
            dve.wait_ge(s_x3, 1)
            add_chunks(1)


FEATURES = np.concatenate([MUL + np.arange(3 * MUL).reshape(MUL, 3).T.ravel(), np.arange(MUL)])


def weight_order():
    cols = np.arange(W_NUMEL).reshape(4, MUL, MUL)
    w_000, w_011, w_101, w_110 = (c.T for c in cols)
    return np.concatenate([np.concatenate([w_000, w_110], axis=1).ravel(), w_011.ravel(), w_101.ravel()])


def kernel(x, src, dst, edge_attr_32, edge_attr_4, L0_gnn_W1, L0_gnn_b1, L0_gnn_W2, L0_gnn_b2,
           L0_gnn_si_w0, L0_gnn_si_w1, L1_gnn_eps):
    import concourse.bacc as bacc
    from concourse.bass_utils import run_bass_kernel_spmd

    def padded(a, n, value=0):
        a = np.asarray(a)
        out = np.full((n,) + a.shape[1:], value, a.dtype)
        out[:a.shape[0]] = a
        return out

    order = weight_order()
    dst_p = padded(dst, EDGES, NODES - 1)
    arrays = {
        "x": padded(x, NODES)[:, FEATURES].reshape(P, SLOTS, D),
        "src": padded(src, EDGES).reshape(GROUPS, P, TILES),
        "dst_groups": dst_p.reshape(PAIRS, 2, GROUP),
        "dst_tiles": dst_p.reshape(GROUPS, P, TILES).transpose(1, 0, 2).reshape(P, GROUPS * TILES),
        "edge_t": padded(edge_attr_32, EDGES).reshape(GROUPS, P, SUBS, TILES // SUBS, D_EDGE)
        .transpose(0, 2, 4, 3, 1).reshape(GROUPS, P, SUB),
        "sh": padded(edge_attr_4, EDGES).reshape(GROUPS, P, TILES, 4),
        "w1": np.asarray(L0_gnn_W1),
        "b1": np.asarray(L0_gnn_b1).reshape(D_MLP, 1),
        "w2": np.asarray(L0_gnn_W2)[:, order],
        "b2": np.asarray(L0_gnn_b2)[order].reshape(1, W_NUMEL),
        "si0": np.asarray(L0_gnn_si_w0),
        "si1": np.asarray(L0_gnn_si_w1),
        "eps": np.asarray(L1_gnn_eps).reshape(1, 1),
    }
    nc = bacc.Bacc("TRN2", target_bir_lowering=False, num_devices=1)
    args, ins = [], {}
    for name, a in arrays.items():
        a = np.ascontiguousarray(a)
        ins[f"in_{name}"] = a
        args.append(nc.dram_tensor(f"in_{name}", a.shape, mybir.dt.from_np(a.dtype),
                                   kind="ExternalInput").ap())
    args.append(nc.dram_tensor("out_nodes", (P, SLOTS, D), F32, kind="ExternalOutput").ap())
    build(nc, *args)
    r = run_bass_kernel_spmd(nc, [ins], core_ids=[0])
    got = r.results[0]["out_nodes"].reshape(NODES, D)[:N_NODES]
    back = np.empty(D, np.int64)
    back[FEATURES] = np.arange(D)
    return np.ascontiguousarray(got[:, back])
```

```python
from contextlib import ExitStack

import numpy as np

import concourse.bass as bass
from concourse import mybir
from concourse.alu_op_type import AluOpType as ALU

F32 = mybir.dt.float32
I32 = mybir.dt.int32
BF16 = mybir.dt.bfloat16
F16 = mybir.dt.float16
ACT = mybir.ActivationFunctionType
AX = mybir.AxisListType

P = 128
N_NODES, D = 12500, 32
N_EDGES, D_EDGE, D_MLP, MUL = 200000, 32, 64, 8
SLOTS = -(-N_NODES // P)
NODES = SLOTS * P
TILES = 8
GROUP = TILES * P
QUAD = TILES // 2 * P
SUBS = P // D_EDGE
SUB = GROUP // SUBS
GROUPS = 2 * -(-N_EDGES // (2 * GROUP))
EDGES = GROUPS * GROUP
PAIRS = GROUPS // 2
WIN = P
W_NUMEL = 4 * MUL * MUL
ALPHA = 0.25
C110 = 1.0 / float(np.sqrt(3.0))
SI_SCALE = 1.0 / float(np.sqrt(MUL))
EPS = 1e-5
CHUNK = 16
CHUNKS = -(-SLOTS // CHUNK)
PARTS = 3
SPLIT = PARTS * D
SPAN = 14
BANK = 512
SLOTS_BANK = -(-SLOTS // 3)
BANK_KEYS = SLOTS_BANK * SPAN
COUNTED = 3 * BANK_KEYS
CTILES = TILES - 1
SPREAD = CTILES * SPAN
ROW = 16
FAR_COL, ANY_COL, LO_COL = 2, 6, 8
KEYED = 4
AHEAD = 2
OUT_DVE = (1, 4)
ADD_AT = 5
WINDOWS_AT = TILES // 2 - 1
PIECES = [SLOTS * t // CTILES for t in range(CTILES + 1)]


def build(nc, x, src, src_last, src_counted, dst_counted, dst_groups, dst_tiles, edge_t, sh, w1, b1, w2, b2, si0, si1, eps, out):
    table_1 = nc.dram_tensor("table_1", (NODES, D), F32).ap()
    table_2 = nc.dram_tensor("table_2", (NODES, SPLIT), BF16).ap()
    group_table = nc.dram_tensor("group_table", (PAIRS * ROW,), I32).ap()

    ctx = ExitStack()
    with ctx:
        def sb(name, shape, dt=F32):
            return ctx.enter_context(nc.sbuf_tensor(name, shape, dt))

        def ps(name, shape):
            return ctx.enter_context(nc.psum_tensor(name, shape, F32))

        def sem(name):
            return ctx.enter_context(nc.semaphore(name))

        x_nm = sb("x_nm", [P, SLOTS, D])
        by_node = lambda ap: ap.rearrange("p (s d) -> p s d", d=D)
        space_nodes = sb("space_nodes", [P, 2 * SLOTS * D])
        space_edges = sb("space_edges", [P, max(CTILES * COUNTED // 2, 5120)])
        h_nm = by_node(space_nodes[:, 0:SLOTS * D])
        scratch = by_node(space_nodes[:, SLOTS * D:])
        counts = [space[:, 0:CTILES * COUNTED // 2].bitcast(BF16)
                  .rearrange("p (s t n) -> p s t n", t=CTILES, n=SPAN)
                  for space in (space_nodes, space_edges)]
        h_split = sb("h_split", [P, SLOTS, SPLIT], BF16)
        dst_g = h_split[0:PAIRS, :, :].rearrange("p s d -> p (s d)").bitcast(I32)[:, 0:2 * GROUP]\
            .rearrange("p (j e) -> p j e", j=2)
        stat = sb("stat", [P, 4, SLOTS])
        eps_ln = sb("eps_ln", [P, 1])
        eps_gin = sb("eps_gin", [P, 1])
        one_plus_eps = sb("one_plus_eps", [P, 1])
        iota_i = sb("iota_i", [P, P], I32)
        neg_iota = sb("neg_iota", [P, P])
        identity = sb("identity", [P, P])
        w1_sb = sb("w1_sb", [P, SUBS, D_MLP])
        b1_sb = sb("b1_sb", [D_MLP, 1])
        w2_sb = sb("w2_sb", [P, W_NUMEL])
        si_sb = sb("si_sb", [P, P])
        h_t = sb("h_t", [P, 2, P])
        lo_hi = sb("lo_hi", [PAIRS, 2, 2])
        tile_lo_hi = sb("tile_lo_hi", [PAIRS, 2, TILES])
        tile_past = sb("tile_past", [PAIRS, TILES + 1])
        base_flag = sb("base_flag", [PAIRS, ROW], I32)
        table = sb("table", [P, PAIRS, ROW], I32)
        flags = [sb(f"flags{k}", [1, PAIRS, 2]) for k in range(2)]
        fallback_flags = sb("fallback_flags", [1, PAIRS])
        fallback_upto = sb("fallback_upto", [1, PAIRS])
        fallback_rows = sb("fallback_rows", [1, PAIRS], I32)
        ones_row = sb("ones_row", [1, GROUPS])
        far_upto = [sb(f"far_upto{k}", [1, GROUPS]) for k in range(2)]
        past = sb("past", [PAIRS, 2])
        far_rounds = [sb(f"far_rounds{k}", [1, GROUPS], I32) for k in range(2)]
        dst_i = sb("dst_i", [P, GROUPS * TILES], I32)
        neg_loc = sb("neg_loc", [P, GROUPS * TILES])
        src_c = sb("src_c", [P, PAIRS * TILES], I32)
        dst_c = sb("dst_c", [P, PAIRS * TILES], I32)
        src_part = sb("src_part", [P, PAIRS * TILES + AHEAD])
        key = sb("key", [P, PAIRS * TILES + AHEAD])
        iota_part = sb("iota_part", [P, P], F16)
        iota_key = sb("iota_key", [P, COUNTED], F16)
        is_part = [sb(f"is_part{b}", [P, P], BF16) for b in range(KEYED)]
        space_keys = sb("space_keys", [P, KEYED * COUNTED // 2])
        is_key = [space_keys[:, b * COUNTED // 2:(b + 1) * COUNTED // 2].bitcast(BF16)
                  for b in range(KEYED)]
        taken = [0]

        def in_keys(*shape):
            a, n = taken[0], int(np.prod(shape))
            taken[0] = a + n
            dims = " ".join(f"d{k}" for k in range(len(shape)))
            sizes = {f"d{k}": v for k, v in enumerate(shape)}
            return space_keys[:, a:a + n].rearrange(f"p ({dims}) -> p {dims}", **sizes)

        counted_sb = [sb(f"counted_sb{u}", [SPREAD, SPLIT]) for u in range(2)]
        tile_iota = sb("tile_iota", [SPREAD, CTILES], I32)
        tile_below = sb("tile_below", [SPREAD, CTILES])
        tile_mask = sb("tile_mask", [SPREAD, CTILES])
        tile_node = sb("tile_node", [SPREAD, CTILES])
        node_in_tile = sb("node_in_tile", [SPREAD, 1])
        column = sb("column", [SPREAD, PAIRS])
        of_tile_sb = sb("of_tile_sb", [SPREAD, PAIRS, CTILES])
        place = [sb(f"place{u}", [SPREAD, WIN]) for u in range(2)]
        z_split = [sb(f"z_split{u}", [P, TILES + 1, SPLIT], BF16) for u in range(2)]
        z_fallback = sb("z_fallback", [P, TILES, SPLIT], BF16)
        idx_last = [sb(f"idx_last{u}", [P, 1], I32) for u in range(2)]
        last_loc = sb("last_loc", [P, PAIRS])
        idx_fallback = sb("idx_fallback", [P, TILES], I32)
        stack_identity = sb("stack_identity", [SPLIT, D])
        idx = [sb(f"idx{j}", [P, TILES], I32) for j in range(2)]
        z = [rows[:, :, :].rearrange("p t d -> p (t d)").bitcast(F32)[:, 0:TILES * D]
             .rearrange("p (t d) -> p t d", d=D) for rows in z_split]
        sh_sb = [sb(f"sh{j}", [P, TILES, 4]) for j in range(2)]
        edge_sb = [in_keys(SUB) for j in range(2)]
        hid = [space_edges[:, q * QUAD:(q + 1) * QUAD] for q in range(2)]
        onehot = [sb(f"onehot{j}", [P, TILES, WIN]) for j in range(2)]
        msg = [in_keys(TILES, D) for j in range(2)]
        onehot_2 = [oh[:, :, :].rearrange("p t n -> p (t n)")[:, 0:(TILES + 1) * WIN // 2].bitcast(BF16)
                    .rearrange("p (t n) -> p t n", n=WIN) for oh in onehot]
        distance = space_edges[:, 1024:2048].rearrange("p (t n) -> p t n", n=WIN)
        z_v = in_keys(2, 3, TILES // 2, MUL)
        z_s = in_keys(TILES, 2 * MUL)
        v_sh = in_keys(TILES, MUL, 3)
        products_a, products_bc = space_edges[:, 2048:3072], space_edges[:, 3072:5120]
        prod_a = [space_edges[:, 2048 + 512 * q:2560 + 512 * q]
                  .rearrange("p (t o i) -> p t o i", o=MUL, i=2 * MUL) for q in range(2)]
        prod_bc = [space_edges[:, 3072 + 1024 * q:4096 + 1024 * q]
                   .rearrange("p (t c o i) -> p t c o i", c=4, o=MUL, i=MUL) for q in range(2)]
        iota_key_i = h_split[:, :, :].rearrange("p s d -> p (s d)")[:, 4 * GROUP:4 * GROUP + 2 * COUNTED]\
            .bitcast(I32)
        key_tmp = [space_edges[:, 1024 + 800 * n:1024 + 800 * n + PAIRS * TILES] for n in range(4)]
        sums = in_keys(TILES, 4, MUL)
        p_sh = in_keys(TILES, 3, MUL)
        far = sb("far", [P, TILES])
        onehot_far = [sb("onehot_far", [P, TILES, WIN])]
        onehot_far.append(onehot_far[0][:, 0:TILES // 2, :].rearrange("p t n -> p (t n)")
                          .bitcast(BF16).rearrange("p (t n) -> p t n", n=WIN))
        rows_of = [slice(0, D), slice(0, SPLIT)]
        acc_sb = sb("acc_sb", [SPLIT, NODES + WIN])
        acc = [acc_sb[rows_of[k], :] for k in range(2)]

        banks = [ps(f"banks{q}", [P, 3 * BANK]) for q in range(2)]
        w_ps = [b[:, 0:2 * BANK].rearrange("p (t n) -> p t n", n=W_NUMEL) for b in banks]
        hid_ps = [b[:, 2 * BANK:] for b in banks]
        counts_ps = [b[:, :].rearrange("p (b n) -> p b n", n=BANK) for b in banks]
        win_bank = ps("win_bank", [P, BANK])
        win_ps = win_bank[:, 0:WIN]
        counted_win_ps = win_bank[rows_of[1], WIN:2 * WIN]
        last_bank = ps("last_bank", [P, BANK])
        far_ps = [last_bank[rows_of[0], 0:WIN], win_ps[rows_of[1], :]]
        counted_ps = last_bank[0:SPREAD, 0:SPLIT]

        s_x = sem("s_x")
        s_weights = sem("s_weights")
        s_dst = sem("s_dst")
        s_group_out = sem("s_group_out")
        s_group_in = sem("s_group_in")
        s_si = sem("s_si")
        s_iota = sem("s_iota")
        s_iota_f = sem("s_iota_f")
        s_ident = sem("s_ident")
        s_zero = sem("s_zero")
        s_ones = sem("s_ones")
        s_lo_hi = sem("s_lo_hi")
        s_past = sem("s_past")
        s_w2 = sem("s_w2")
        s_inv = sem("s_inv")
        s_flags = sem("s_flags")
        s_eps = sem("s_eps")
        s_base = sem("s_base")
        s_tables = sem("s_tables")
        s_ln = sem("s_ln")
        s_sq = sem("s_sq")
        s_std = sem("s_std")
        s_h = sem("s_h")
        s_table = [sem("s_table1"), sem("s_table2")]
        s_ht = sem("s_ht")
        s_ht_sb = sem("s_ht_sb")
        s_si_mm = sem("s_si_mm")
        s_x1 = sem("s_x1")
        s_nm = [sem("s_nm1"), sem("s_nm2")]
        s_nm_add = [sem("s_nm_add1"), sem("s_nm_add2")]
        s_x3 = sem("s_x3")
        s_out = sem("s_out")
        s_idx = [[sem(f"s_idx{k}{j}") for j in range(2)] for k in range(2)]
        s_z = [[sem(f"s_z{k}{j}") for j in range(2)] for k in range(2)]
        s_sh = [sem(f"s_sh{j}") for j in range(2)]
        s_edge = [sem(f"s_edge{j}") for j in range(2)]
        s_hid_mm = sem("s_hid_mm")
        s_hid = sem("s_hid")
        s_w_mm = sem("s_w_mm")
        s_onehot = [sem(f"s_onehot{k}") for k in range(2)]
        s_vsh = sem("s_vsh")
        s_zs = sem("s_zs")
        s_scaled = sem("s_scaled")
        s_distance = sem("s_distance")
        s_hid_rows = sem("s_hid_rows")
        s_prod_bc = sem("s_prod_bc")
        s_prod = sem("s_prod")
        s_sum_bc = sem("s_sum_bc")
        s_sum_a = sem("s_sum_a")
        s_p_sh = sem("s_p_sh")
        s_msg = sem("s_msg")
        s_win = [sem(f"s_win{k}") for k in range(2)]
        s_acc = [sem(f"s_acc{k}") for k in range(2)]
        s_started = sem("s_started")
        s_far_done = sem("s_far_done")
        s_far_dst = [sem(f"s_far_dst{k}") for k in range(2)]
        s_far_onehot = [sem(f"s_far_onehot{k}") for k in range(2)]
        s_far_win = [sem(f"s_far_win{k}") for k in range(2)]
        s_far_acc = [sem(f"s_far_acc{k}") for k in range(2)]

        s_counted_in = sem("s_counted_in")
        s_iota_key = sem("s_iota_key")
        s_source = sem("s_source")
        s_keys = sem("s_keys")
        s_column = sem("s_column")
        s_var = sem("s_var")
        s_stack = sem("s_stack")
        s_rezero = sem("s_rezero")
        s_split = sem("s_split")
        s_keyed = sem("s_keyed")
        s_counts_mm = sem("s_counts_mm")
        s_counts_out = sem("s_counts_out")
        s_counts_dve = sem("s_counts_dve")
        s_counted = sem("s_counted")
        s_counted_sb = sem("s_counted_sb")
        s_counted_acc = sem("s_counted_acc")
        s_place = sem("s_place")
        s_counted_win = sem("s_counted_win")
        s_fallback_z = sem("s_fallback_z")

        block = ctx.enter_context(nc.Block())

        @block.sync
        def _(sp):
            sp.dma_start(x_nm[:, :, :], x).then_inc(s_x, 16)
            sp.dma_start(eps_gin[:, :], eps.to_broadcast([P, 1])).then_inc(s_weights, 16)
            sp.dma_start(b1_sb[:, :], b1).then_inc(s_weights, 16)
            sp.dma_start(dst_g[:, :, :], dst_groups).then_inc(s_dst, 16)
            sp.dma_start(dst_i[:, :], dst_tiles).then_inc(s_dst, 16)
            sp.dma_start(src_c[:, :], src_counted).then_inc(s_counted_in, 16)
            sp.dma_start(dst_c[:, :], dst_counted).then_inc(s_counted_in, 16)
            sp.wait_ge(s_zero, 3)
            for b in range(P // MUL):
                sp.dma_start(si_sb[b * MUL:(b + 1) * MUL, b * MUL:(b + 1) * MUL],
                             si0 if b % 4 == 3 else si1).then_inc(s_si, 16)

            for b in range(SUBS):
                sp.dma_start(w1_sb[b * D_EDGE:(b + 1) * D_EDGE, b, :], w1).then_inc(s_weights, 16)
            sp.dma_start(w2_sb[0:D_MLP, :], w2).then_inc(s_weights, 16)
            sp.dma_start(w2_sb[D_MLP:D_MLP + 1, :], b2).then_inc(s_weights, 16)

            def loads(g, i, j, first):
                if not first:
                    sp.wait_ge(s_z[0][j], 16 * TILES * i)
                sp.dma_start(idx[j][:, :], src[g, :, :]).then_inc(s_idx[0][j], 16)
                if not first:
                    sp.wait_ge(s_hid_mm, 2 * g - 2)
                sp.dma_start(edge_sb[j][:, :], edge_t[g, :, :]).then_inc(s_edge[j], 16)
                if not first:
                    sp.wait_ge(s_msg, g - 1)
                sp.dma_start(sh_sb[j][:, :, :], sh[g, :, :, :]).then_inc(s_sh[j], 16)

            for j in range(2):
                loads(j, 0, j, True)
            sp.wait_ge(s_h, 1)
            sp.dma_start(table_1.rearrange("(p s) d -> p s d", s=SLOTS), h_nm[:, :, :])\
              .then_inc(s_table[0], 16)
            sp.wait_ge(s_base, 6)
            sp.dma_start(group_table.rearrange("(p n) -> p n", n=ROW), base_flag[:, :]).then_inc(s_group_out, 16)
            sp.wait_ge(s_group_out, 16)
            sp.dma_start(table[:, :, :].rearrange("p a b -> p (a b)"),
                         group_table.partition_broadcast(P)).then_inc(s_group_in, 16)
            with sp.Fori(1, PAIRS) as i:
                for j in range(2):
                    loads(2 * i + j, i, j, False)
            for u in range(2):
                sp.wait_ge(s_z[0][u], 16 * TILES * PAIRS)
                sp.dma_start(idx[u][:, :], src[2 * u, :, :]).then_inc(s_idx[1][u], 16)
            for c in range(CHUNKS):
                a, b = c * CHUNK, min((c + 1) * CHUNK, SLOTS)
                sp.wait_ge(s_split, 4 * (c + 1))
                sp.dma_start(table_2.rearrange("(p s) d -> p s d", s=SLOTS)[:, a:b, :],
                             h_split[:, a:b, :]).then_inc(s_table[1], 16)

            def last_tile(n, u):
                sp.dma_start(idx_last[u][:, :], src_last[2 * n + u - 2, :, :])\
                  .then_inc(s_idx[1][u], 16)

            with sp.Fori(1, PAIRS // 2) as n:
                for u in range(2):
                    sp.wait_ge(s_z[1][u], 16 * ((TILES + 1) * n - 1))
                    sp.dma_start(idx[u][:, :], src[4 * n + 2 * u, :, :]).then_inc(s_idx[1][u], 16)
                    last_tile(n, u)
            for u in range(2):
                sp.wait_ge(s_z[1][u], 16 * ((TILES + 1) * (PAIRS // 2) - 1))
                last_tile(PAIRS // 2, u)
            for c in range(CHUNKS):
                a, b = c * CHUNK, min((c + 1) * CHUNK, SLOTS)
                sp.wait_ge(s_nm_add[1], c + 1)
                sp.dma_start(out[:, a:b, :], x_nm[:, a:b, :]).then_inc(s_out, 16)
            sp.wait_ge(s_out, 16 * CHUNKS)

        @block.gpsimd
        def _(pool):
            pool.iota(iota_i[:, :], pattern=[[1, P]], base=0, channel_multiplier=0).then_inc(s_iota, 1)
            pool.iota(iota_key_i, pattern=[[1, COUNTED]], base=0, channel_multiplier=0)\
                .then_inc(s_iota, 1)
            pool.iota(tile_iota[:, :], pattern=[[-SPAN, CTILES]], base=0, channel_multiplier=1)\
                .then_inc(s_iota, 1)
            pool.memset(identity[:, :], 0.0).then_inc(s_ident, 1)
            pool.memset(si_sb[:, :], 0.0).then_inc(s_zero, 1)
            pool.memset(w1_sb[:, :, :], 0.0).then_inc(s_zero, 1)
            pool.memset(w2_sb[:, :], 0.0).then_inc(s_zero, 1)
            pool.wait_ge(s_ident, 1)
            pool.affine_select(out=identity[:, :], in_=identity[:, :], compare_op=ALU.not_equal,
                               fill=1.0, base=0, pattern=[[-1, P]], channel_multiplier=1)\
                .then_inc(s_ident, 1)
            pool.memset(acc_sb[:, :], 0.0).then_inc(s_zero, 1)

            source, end, off, late = key_tmp
            quotient, keys = src_part[:, 0:PAIRS * TILES], key[:, 0:PAIRS * TILES]
            by_tile = lambda ap: ap.rearrange("p (g t) -> p g t", t=TILES)
            pool.memset(src_part[:, PAIRS * TILES:], 0.0)
            pool.memset(key[:, PAIRS * TILES:], 0.0)
            pool.wait_ge(s_counted_in, 32)
            pool.tensor_copy(source, src_c[:, :])
            pool.drain()
            pool.tensor_scalar(off, source, 1.0 / SLOTS, None, ALU.mult)
            pool.drain()
            pool.tensor_copy(late.bitcast(I32), off)
            pool.drain()
            pool.tensor_copy(quotient, late.bitcast(I32))
            pool.drain()
            pool.tensor_scalar(keys, quotient, -float(SLOTS), None, ALU.mult)
            pool.drain()
            pool.tensor_tensor(keys, keys, source, ALU.add).then_inc(s_source, 1)

            def gather(k, table_dram, z, i, j):
                pool.wait_ge(s_idx[k][j], 16 * (i + 1))
                pool.sem_inc(s_started, 1)
                for t in range(TILES):
                    pool.indirect_dma_start(
                        out=z[j][:, t, :], out_offset=None, in_=table_dram,
                        in_offset=bass.IndirectOffsetOnAxis(ap=idx[j][:, t:t + 1], axis=0),
                    ).then_inc(s_z[k][j], 16)

            pool.wait_ge(s_table[0], 16)
            for j in range(2):
                gather(0, table_1, z, 0, j)
            with pool.Fori(1, PAIRS) as i:
                for j in range(2):
                    pool.wait_ge(s_prod, 2 * (2 * i + j) - 2)
                    gather(0, table_1, z, i, j)
            pool.wait_ge(s_msg, GROUPS)
            pool.wait_ge(s_tables, 4)
            pool.wait_ge(s_source, 1)
            pool.tensor_scalar(late, keys, float(SLOTS), None, ALU.is_ge)
            pool.tensor_scalar(off, keys, 0.0, None, ALU.is_lt)
            pool.drain()
            pool.tensor_tensor(off, off, late, ALU.subtract)
            pool.drain()
            pool.tensor_tensor(quotient, quotient, off, ALU.subtract)
            pool.tensor_scalar(source, off, float(SLOTS), None, ALU.mult)
            pool.drain()
            pool.tensor_tensor(keys, keys, source, ALU.add)
            pool.drain()
            least, within = source, late
            pool.tensor_scalar(keys, keys, float(SPAN), 1.0, ALU.mult, ALU.add)
            pool.tensor_copy(end, dst_c[:, :])
            pool.tensor_copy(by_tile(least), table[:, :, LO_COL:LO_COL + TILES])
            pool.drain()
            pool.tensor_tensor(off, end, least, ALU.subtract)
            pool.drain()
            pool.tensor_tensor(keys, keys, off, ALU.add)
            pool.tensor_scalar(within, off, float(SPAN), None, ALU.is_lt)
            pool.drain()
            pool.tensor_tensor(keys, keys, within, ALU.mult)
            pool.tensor_copy(by_tile(least), table[:, :, 1:2].broadcast_to([P, PAIRS, TILES]))
            pool.drain()
            pool.tensor_tensor(off, end, least, ALU.subtract)
            pool.drain()
            pool.tensor_scalar(within, off, float(WIN), None, ALU.is_lt)
            pool.drain()
            pool.tensor_tensor(keys, keys, within, ALU.mult)
            pool.drain()
            pool.tensor_scalar(keys, keys, -1.0, None, ALU.add).then_inc(s_keys, 1)
            pool.drain()
            pool.tensor_scalar(by_tile(within)[:, :, CTILES], by_tile(keys)[:, :, CTILES], 0.0, None,
                               ALU.is_ge)
            pool.tensor_scalar(last_loc[:, :], by_tile(off)[:, :, CTILES], 1.0, None, ALU.add)
            pool.drain()
            pool.tensor_tensor(last_loc[:, :], last_loc[:, :], by_tile(within)[:, :, CTILES], ALU.mult)
            pool.drain()
            pool.tensor_scalar(last_loc[:, :], last_loc[:, :], -1.0, None, ALU.add).then_inc(s_keys, 1)
            pool.wait_ge(s_nm[0], CHUNKS)
            pool.memset(acc[0], 0.0).then_inc(s_rezero, 1)
            pool.wait_ge(s_table[1], 16 * CHUNKS)

            def fallback(i):
                flag = pool.value_load(table[0:1, i, FAR_COL + 3:FAR_COL + 4], min_val=0, max_val=1)
                with pool.If(flag):
                    rows = pool.value_load(fallback_rows[0:1, bass.ds(i, 1)], min_val=0,
                                           max_val=16 * TILES * PAIRS)
                    if not isinstance(i, int) or i >= 1:
                        pool.wait_ge(s_win[1], i)
                        pool.sem_inc(s_started, 1)
                    pool.tensor_copy(idx_fallback[:, :], src_c[:, bass.ds(i * TILES, TILES)])
                    pool.drain()
                    for t in range(TILES):
                        pool.indirect_dma_start(
                            out=z_fallback[:, t, :], out_offset=None, in_=table_2,
                            in_offset=bass.IndirectOffsetOnAxis(ap=idx_fallback[:, t:t + 1], axis=0),
                        ).then_inc(s_fallback_z, 16)
                    pool.wait_ge(s_fallback_z, rows + 16 * TILES)
                    pool.sem_inc(s_started, 1)

            def gather_pair(n, u):
                pool.wait_ge(s_idx[1][u], 16 * (2 * n + 1))
                pool.sem_inc(s_started, 1)
                for t in range(TILES):
                    pool.indirect_dma_start(
                        out=z_split[u][:, t, :], out_offset=None, in_=table_2,
                        in_offset=bass.IndirectOffsetOnAxis(ap=idx[u][:, t:t + 1], axis=0),
                    ).then_inc(s_z[1][u], 16)

            def gather_last(u):
                pool.indirect_dma_start(
                    out=z_split[u][:, TILES, :], out_offset=None, in_=table_2,
                    in_offset=bass.IndirectOffsetOnAxis(ap=idx_last[u][:, 0:1], axis=0),
                ).then_inc(s_z[1][u], 16)

            for i in range(4):
                if i >= 2:
                    pool.wait_ge(s_win[1], i - 1)
                gather_pair(i // 2, i % 2)
                if i >= 2:
                    gather_last(i % 2)
                fallback(i)
            with pool.Fori(2, PAIRS // 2) as n:
                for u in range(2):
                    pool.wait_ge(s_win[1], 2 * n + u - 1)
                    pool.sem_inc(s_started, 1)
                    pool.wait_ge(s_counted_win, 2 * n + u - 3)
                    pool.sem_inc(s_started, 1)
                    gather_pair(n, u)
                    gather_last(u)
                    fallback(2 * n + u)
            for u in range(2):
                pool.wait_ge(s_counted_win, PAIRS + u - 3)
                pool.sem_inc(s_started, 1)
                pool.wait_ge(s_idx[1][u], 16 * PAIRS)
                pool.sem_inc(s_started, 1)
                gather_last(u)

        @block.scalar
        def _(act):
            def norm(k):
                act.wait_ge(s_ln, 3 * k + 2)
                act.activation(scratch[:, :, :], h_nm[:, :, :], ACT.Square).then_inc(s_sq, 1)
                act.wait_ge(s_ln, 3 * k + 3)
                act.wait_ge(s_eps, 1)
                act.activation(stat[:, 2, :], stat[:, 1, :], ACT.Sqrt, bias=eps_ln[:, :],
                               scale=1.0 / D).then_inc(s_std, 1)

            norm(0)
            for n in range(-(-SLOTS // 4)):
                rows = min(4, SLOTS - 4 * n) * D
                act.wait_ge(s_ht, n + 1)
                if n >= 2:
                    act.wait_ge(s_si_mm, n - 1)
                act.activation(h_t[0:rows, n % 2, :], hid_ps[n % 2][0:rows, 0:P], ACT.Copy,
                               scale=SI_SCALE).then_inc(s_ht_sb, 1)
            act.wait_ge(s_weights, 16 * (SUBS + 4))
            act.wait_ge(s_ones, 2)

            def hidden(g, first):
                for q in range(2):
                    act.wait_ge(s_hid_mm, 2 * g + q + 1)
                    if not first:
                        act.wait_ge(s_w_mm, 2 * g + q - 1)
                    act.activation(hid[q][0:D_MLP, :], hid_ps[q][0:D_MLP, :], ACT.Relu,
                                   bias=b1_sb[:, :]).then_inc(s_hid, 1)

            def one_hot(g, j):
                if not (isinstance(g, int) and g == 0):
                    act.wait_ge(s_onehot[0], g)
                for t in range(TILES):
                    act.activation(distance[:, t, :], neg_iota[:, :], ACT.Abs, scale=-1.0,
                                   bias=neg_loc[:, bass.ds(g * TILES + t, 1)]).then_inc(s_distance, 1)
                if not isinstance(g, int):
                    act.wait_ge(s_win[0], g - 1)
                act.wait_ge(s_distance, TILES * (g + 1))
                act.activation(onehot[j][:, :, :], distance[:, :, :], ACT.Relu, bias=1.0,
                               scale=-1.0).then_inc(s_onehot[0], 1)

            def scaled(g, i, j):
                act.wait_ge(s_z[0][j], 16 * TILES * (i + 1))
                act.wait_ge(s_sh[j], 16 * (i + 1))
                if not (isinstance(g, int) and g == 0):
                    act.wait_ge(s_prod, 2 * g)
                for t in range(TILES):
                    act.activation(z_v[:, t // 4, :, t % 4, :],
                                   z[j][:, t, 0:3 * MUL].rearrange("p (m i) -> p m i", m=3), ACT.Copy,
                                   scale=sh_sb[j][:, t, 0:1]).then_inc(s_scaled, 1)

            hidden(0, True)
            scaled(0, 0, 0)
            act.wait_ge(s_tables, 4)
            act.wait_ge(s_iota_f, 1)
            act.wait_ge(s_source, 1)
            one_hot(0, 0)
            hidden(1, False)
            one_hot(1, 1)
            scaled(1, 0, 1)
            with act.Fori(1, PAIRS) as i:
                for j in range(2):
                    hidden(2 * i + j, False)
                    one_hot(2 * i + j, j)
                    scaled(2 * i + j, i, j)
            def deviation(c):
                a, b = c * CHUNK, min((c + 1) * CHUNK, SLOTS)
                act.wait_ge(s_var, c + 1)
                act.activation(stat[:, 2, a:b], stat[:, 1, a:b], ACT.Sqrt, bias=eps_ln[:, :],
                               scale=1.0 / D).then_inc(s_std, 1)

            for c in range(CHUNKS):
                a, b = c * CHUNK, min((c + 1) * CHUNK, SLOTS)
                act.wait_ge(s_ln, 3 + 2 * (c + 1))
                act.activation(scratch[:, a:b, :], h_nm[:, a:b, :], ACT.Square).then_inc(s_sq, 1)
                if c >= 1:
                    deviation(c - 1)
            deviation(CHUNKS - 1)

            def counted_out(i, u):
                act.wait_ge(s_counted, i - 1)
                if not isinstance(i, int) or i >= 4:
                    act.wait_ge(s_counted_win, i - 3)
                act.activation(counted_sb[u][:, :], counted_ps, ACT.Copy).then_inc(s_counted_sb, 1)

            def counts_out(i, u):
                if not isinstance(i, int) or i >= 2:
                    counted_out(i, u)
                for t in range(CTILES):
                    b = 2 if t in OUT_DVE else 3
                    act.wait_ge(s_counts_mm, CTILES * i + t + 1)
                    act.activation(
                        counts[u][:, 0:b * SLOTS_BANK, t, :].rearrange("p (b s) n -> p b s n", b=b),
                        counts_ps[(u + t) % 2][:, 0:b, 0:BANK_KEYS].rearrange("p b (s n) -> p b s n", n=SPAN),
                        ACT.Copy).then_inc(s_counts_out, 1)

            act.wait_ge(s_x3, CHUNKS)
            counts_out(0, 0)
            act.wait_ge(s_w_mm, 2 * GROUPS)
            act.wait_ge(s_onehot[0], GROUPS)
            for i in range(1, 4):
                counts_out(i, i % 2)
            with act.Fori(2, PAIRS // 2) as n:
                for u in range(2):
                    counts_out(2 * n + u, u)
            for u in range(2):
                counted_out(PAIRS + u, u)

        @block.tensor
        def _(pe):
            def far_sums(k, i, j, rows, group):
                flag = pe.value_load(table[0:1, i, FAR_COL + 2 * k + j:FAR_COL + 2 * k + j + 1],
                                     min_val=0, max_val=1)
                with pe.If(flag):
                    done = pe.value_load(far_rounds[k][0:1, bass.ds(group, 1)], min_val=0,
                                         max_val=GROUPS * SLOTS)
                    if k == 1 and j == 1:
                        gathered = pe.value_load(fallback_rows[0:1, bass.ds(i, 1)], min_val=0,
                                                 max_val=16 * TILES * PAIRS)
                        pe.wait_ge(s_fallback_z, gathered + 16 * TILES)
                        pe.sem_inc(s_far_done, 1)
                    with pe.Fori(0, SLOTS) as w:
                        pe.wait_ge(s_far_onehot[k], done + w + 1)
                        pe.wait_ge(s_far_acc[k], done + w + 1)
                        for t in range(TILES):
                            mm = pe.matmul(far_ps[k], rows[:, t, :], onehot_far[k][:, t, :],
                                           start=(t == 0), stop=(t == TILES - 1))
                        mm.then_inc(s_far_win[k], 1)
                    if k == 1:
                        pe.wait_ge(s_far_acc[k], done + SLOTS + 1)
                        pe.sem_inc(s_far_done, 1)

            def window_sums(k, rows, onehot):
                for t in range(TILES):
                    mm = pe.matmul(win_ps[rows_of[k], :], rows[:, t, :], onehot[:, t, :],
                                   start=(t == 0), stop=(t == TILES - 1))
                mm.then_inc(s_win[k], 1)

            def to_node_major(k):
                turn = identity[rows_of[0], rows_of[0]] if k == 0 else stack_identity[:, :]
                for c in range(CHUNKS):
                    if c >= 2:
                        pe.wait_ge(s_nm_add[k], c - 1)
                    nm = w_ps[c % 2][:, 0:2, :].rearrange("p a (s d) -> p (a s) d", d=D)
                    for s in range(c * CHUNK, min((c + 1) * CHUNK, SLOTS)):
                        mm = pe.matmul(nm[:, s % CHUNK, :], acc[k][:, s:NODES:SLOTS],
                                       turn, start=True, stop=True)
                    mm.then_inc(s_nm[k], 1)

            pe.wait_ge(s_ident, 2)
            pe.wait_ge(s_h, 1)
            pe.wait_ge(s_si, 16 * (P // MUL))
            n_fours = -(-SLOTS // 4)

            def self_product(n):
                rows = min(4, SLOTS - 4 * n) * D
                c = n // 4
                nm = w_ps[c % 2][:, 0:2, :].rearrange("p a d -> p (a d)")
                pe.wait_ge(s_ht_sb, n + 1)
                if n % 4 == 0 and c >= 2:
                    pe.wait_ge(s_x1, c - 1)
                pe.matmul(nm[:, (n % 4) * P:(n % 4) * P + rows], h_t[0:rows, n % 2, :],
                          si_sb[0:rows, 0:rows], start=True, stop=True).then_inc(s_si_mm, 1)

            for n in range(n_fours):
                rows = min(4, SLOTS - 4 * n) * D
                if n >= 2:
                    pe.wait_ge(s_ht_sb, n - 1)
                pe.transpose(hid_ps[n % 2][0:rows, 0:P],
                             h_nm[:, 4 * n:4 * n + rows // D, :].rearrange("p s d -> p (s d)"),
                             identity[:, :]).then_inc(s_ht, 1)
                if n >= 1:
                    self_product(n - 1)
            self_product(n_fours - 1)
            pe.wait_ge(s_w2, 3)
            pe.wait_ge(s_weights, 16 * (SUBS + 4))

            def hidden(g, i, j, first):
                pe.wait_ge(s_edge[j], 16 * (i + 1))
                for q in range(2):
                    if first:
                        pe.wait_ge(s_ht_sb, n_fours)
                    else:
                        pe.wait_ge(s_hid, 2 * g + q - 1)
                    for b in range(2):
                        mm = pe.matmul(hid_ps[q][0:D_MLP, b * SUB:(b + 1) * SUB],
                                       w1_sb[:, 2 * q + b, :], edge_sb[j][:, :], start=True, stop=True)
                    mm.then_inc(s_hid_mm, 1)

            def weights(g, first):
                for q in range(2):
                    pe.wait_ge(s_hid, 2 * g + q + 1)
                    if first:
                        pe.wait_ge(s_x1, CHUNKS)
                    else:
                        pe.wait_ge(s_prod, 2 * g + q - 1)
                    for t in range(4):
                        mm = pe.matmul(w_ps[q][:, t, :], hid[q][:, t * P:(t + 1) * P], w2_sb[:, :],
                                       start=True, stop=True)
                    mm.then_inc(s_w_mm, 1)

            def trip(i):
                for j in range(2):
                    g = 2 * i + j
                    weights(g, isinstance(i, int) and g == 0)
                    if not (isinstance(i, int) and g == GROUPS - 1):
                        hidden(g + 1, i + j, 1 - j, False)
                    if not (isinstance(i, int) and g == 0):
                        pe.wait_ge(s_msg, g)
                        pe.wait_ge(s_onehot[0], g)
                        far_sums(0, i if j else i - 1, 1 - j, msg[1 - j], g - 1)
                        if not (isinstance(i, int) and g == 1):
                            pe.wait_ge(s_acc[0], g - 1)
                        window_sums(0, msg[1 - j], onehot[1 - j])

            hidden(0, 0, 0, True)
            pe.wait_ge(s_tables, 4)
            trip(0)
            with pe.Fori(1, PAIRS - 1) as i:
                trip(i)
            trip(PAIRS - 1)
            pe.wait_ge(s_msg, GROUPS)
            pe.wait_ge(s_onehot[0], GROUPS)
            far_sums(0, PAIRS - 1, 1, msg[1], GROUPS - 1)
            pe.wait_ge(s_acc[0], GROUPS - 1)
            window_sums(0, msg[1], onehot[1])
            pe.wait_ge(s_acc[0], GROUPS)
            to_node_major(0)

            def counted_sums(i, u, t):
                if t == 0:
                    pe.wait_ge(s_counts_out, CTILES * i)
                    pe.wait_ge(s_counts_dve, len(OUT_DVE) * i)
                    if not isinstance(i, int) or i >= 2:
                        pe.wait_ge(s_counted_sb, i - 1)
                for s in range(PIECES[t], PIECES[t + 1]):
                    mm = pe.matmul(counted_ps, counts[1 - u][:, s, :, :].rearrange("p t n -> p (t n)"),
                                   h_split[:, s, :],
                                   start=(s == 0), stop=(s == SLOTS - 1))
                if t == CTILES - 1:
                    mm.then_inc(s_counted, 1)

            def counted_window(i, u):
                pe.wait_ge(s_counted_sb, i - 1)
                pe.wait_ge(s_place, 2 * (i - 1))
                pe.matmul(counted_win_ps, counted_sb[u][:, :], place[u][:, :], start=True, stop=False)
                pe.matmul(counted_win_ps, z_split[u][:, TILES, :], onehot_2[u][:, TILES, :],
                          start=False, stop=True).then_inc(s_counted_win, 1)

            def second_layer(i, n, u, r):
                for t in range(CTILES):
                    tile, b4 = CTILES * i + t, (CTILES * r + t) % KEYED
                    if t == 0:
                        flag = pe.value_load(table[0:1, i, ANY_COL:ANY_COL + 1], min_val=0, max_val=1)
                    pe.wait_ge(s_keyed, 2 * (tile + 1))
                    if not (isinstance(i, int) and tile < 2):
                        pe.wait_ge(s_counts_out, tile - 1)
                        if (t - 2) % CTILES in OUT_DVE:
                            pe.wait_ge(s_counts_dve, len(OUT_DVE) * (i - (t < 2))
                                       + OUT_DVE.index((t - 2) % CTILES) + 1)
                    for b in range(3):
                        mm = pe.matmul(counts_ps[(u + t) % 2][:, b, 0:BANK_KEYS], is_part[b4][:, :],
                                       is_key[b4][:, b * BANK_KEYS:(b + 1) * BANK_KEYS],
                                       start=True, stop=True)
                    mm.then_inc(s_counts_mm, 1)
                    if not isinstance(i, int) or i >= 1:
                        counted_sums(i, u, t)
                    if t == WINDOWS_AT:
                        pe.wait_ge(s_z[1][u], 16 * ((TILES + 1) * n + TILES))
                        pe.wait_ge(s_onehot[1], TILES // 2 * (i + 1))
                        if not isinstance(i, int) or i >= 1:
                            pe.wait_ge(s_acc[1], i)
                        if not isinstance(i, int) or i >= 3:
                            pe.wait_ge(s_counted_acc, i - 2)
                        with pe.If(flag):
                            far_sums(1, i, 0, z_split[u], 2 * i)
                            far_sums(1, i, 1, z_fallback, 2 * i + 1)
                        window_sums(1, z_split[u], onehot_2[u])
                        if not isinstance(i, int) or i >= 2:
                            counted_window(i, u)

            pe.wait_ge(s_nm_add[0], CHUNKS)
            pe.wait_ge(s_hid, 2 * GROUPS)
            pe.wait_ge(s_split, 4 * CHUNKS)
            for i in range(6):
                second_layer(i, i // 2, i % 2, i % 4)
            with pe.Fori(1, (PAIRS - 2) // 4) as m:
                for k in range(2, 6):
                    second_layer(4 * m + k, 2 * m + k // 2, k % 2, k % 4)
            for t in range(CTILES):
                counted_sums(PAIRS, 0, t)
            pe.wait_ge(s_acc[1], PAIRS)
            for i in (PAIRS, PAIRS + 1):
                pe.wait_ge(s_counted_acc, i - 2)
                pe.wait_ge(s_z[1][i % 2], 16 * (TILES + 1) * (PAIRS // 2))
                counted_window(i, i % 2)
            pe.wait_ge(s_counted_acc, PAIRS)
            to_node_major(1)

        @block.vector
        def _(dve):
            def norm(k):
                dve.tensor_reduce(stat[:, 0, :], x_nm[:, :, :], AX.X, ALU.add).then_inc(s_ln, 1)
                dve.wait_ge(s_ln, 3 * k + 1)
                dve.scalar_tensor_tensor(
                    out=h_nm[:, :, :], in0=stat[:, 0, :].unsqueeze(2).broadcast_to([P, SLOTS, D]),
                    scalar=-1.0 / D, in1=x_nm[:, :, :], op0=ALU.mult, op1=ALU.add).then_inc(s_ln, 1)
                dve.wait_ge(s_sq, k + 1)
                dve.tensor_reduce(stat[:, 1, :], scratch[:, :, :], AX.X, ALU.add).then_inc(s_ln, 1)
                dve.wait_ge(s_std, k + 1)
                dve.reciprocal(stat[:, 3, :], stat[:, 2, :]).then_inc(s_inv, 1)
                dve.wait_ge(s_inv, k + 1)
                dve.scalar_tensor_tensor(
                    out=h_nm[:, :, :], in0=h_nm[:, :, :], scalar=0.0,
                    in1=stat[:, 3, :].unsqueeze(2).broadcast_to([P, SLOTS, D]),
                    op0=ALU.max, op1=ALU.mult).then_inc(s_h, 1)

            for k in range(2):
                dve.sem_inc(s_far_acc[k], 1)
                dve.sem_inc(s_far_win[k], 1)
            dve.memset(eps_ln[:, :], EPS).then_inc(s_eps, 1)
            dve.memset(ones_row[:, :], 1.0).then_inc(s_eps, 1)
            for q in range(2):
                dve.memset(hid[q][D_MLP:, :], 0.0).then_inc(s_hid_rows, 1)
            dve.wait_ge(s_hid_rows, 2)
            for q in range(2):
                dve.memset(hid[q][D_MLP:D_MLP + 1, :], 1.0).then_inc(s_ones, 1)
            dve.wait_ge(s_x, 16)
            norm(0)
            dve.wait_ge(s_dst, 32)
            dve.tensor_reduce(lo_hi[:, :, 0], dst_g[:, :, :], AX.X, ALU.min).then_inc(s_lo_hi, 1)
            dve.tensor_reduce(lo_hi[:, :, 1], dst_g[:, :, :], AX.X, ALU.max).then_inc(s_lo_hi, 1)
            dve.wait_ge(s_lo_hi, 2)
            dve.scalar_tensor_tensor(out=past[:, :], in0=lo_hi[:, :, 1], scalar=float(-WIN),
                                     in1=lo_hi[:, :, 0], op0=ALU.add, op1=ALU.subtract)\
               .then_inc(s_past, 1)
            dve.tensor_copy(base_flag[:, 0:2], lo_hi[:, :, 0]).then_inc(s_base, 1)
            by_tile = dst_g[:, 1, :].rearrange("p (t e) -> p t e", t=TILES)
            dve.tensor_reduce(tile_lo_hi[:, 0, :], by_tile, AX.X, ALU.min).then_inc(s_lo_hi, 1)
            dve.tensor_reduce(tile_lo_hi[:, 1, :], by_tile, AX.X, ALU.max).then_inc(s_lo_hi, 1)
            dve.wait_ge(s_past, 1)
            dve.tensor_scalar(base_flag[:, FAR_COL:FAR_COL + 2], past[:, :], 0.0, None, ALU.is_ge)\
               .then_inc(s_base, 1)
            dve.wait_ge(s_lo_hi, 4)
            dve.tensor_tensor(tile_past[:, 0:TILES], tile_lo_hi[:, 1, :], tile_lo_hi[:, 0, :],
                              ALU.subtract).then_inc(s_past, 1)
            dve.tensor_copy(base_flag[:, LO_COL:LO_COL + TILES], tile_lo_hi[:, 0, :]).then_inc(s_base, 1)
            dve.tensor_scalar(base_flag[:, FAR_COL + 2:FAR_COL + 3], past[:, 0:1], 0.0, None, ALU.is_ge)\
               .then_inc(s_base, 1)
            dve.memset(base_flag[:, ANY_COL + 1:LO_COL], 0.0)
            dve.wait_ge(s_past, 2)
            dve.tensor_reduce(tile_past[:, TILES:], tile_past[:, 0:TILES], AX.X, ALU.max)\
               .then_inc(s_past, 1)
            dve.wait_ge(s_past, 3)
            dve.scalar_tensor_tensor(out=tile_past[:, 0:1], in0=past[:, 1:2], scalar=float(SPAN),
                                     in1=tile_past[:, TILES:], op0=ALU.add, op1=ALU.max)\
               .then_inc(s_past, 1)
            dve.wait_ge(s_past, 4)
            dve.tensor_scalar(base_flag[:, FAR_COL + 3:FAR_COL + 4], tile_past[:, 0:1], float(SPAN),
                              None, ALU.is_ge).then_inc(s_base, 1)
            dve.wait_ge(s_base, 5)
            dve.tensor_tensor(base_flag[:, ANY_COL:ANY_COL + 1],
                              base_flag[:, FAR_COL + 2:FAR_COL + 3],
                              base_flag[:, FAR_COL + 3:FAR_COL + 4], ALU.max).then_inc(s_base, 1)
            dve.wait_ge(s_weights, 16 * (SUBS + 4))
            part_a = w2_sb[:, 0:2 * MUL * MUL].rearrange("k (o i) -> k o i", i=2 * MUL)
            dve.tensor_scalar(part_a[:, :, MUL:], part_a[:, :, MUL:], ALPHA * C110, None, ALU.mult)\
               .then_inc(s_w2, 1)
            dve.tensor_scalar(part_a[:, :, 0:MUL], part_a[:, :, 0:MUL], ALPHA, None, ALU.mult)\
               .then_inc(s_w2, 1)
            dve.tensor_scalar(w2_sb[:, 2 * MUL * MUL:], w2_sb[:, 2 * MUL * MUL:], ALPHA, None, ALU.mult)\
               .then_inc(s_w2, 1)
            dve.tensor_scalar(one_plus_eps[:, :], eps_gin[:, :], 1.0, None, ALU.add).then_inc(s_eps, 1)
            dve.wait_ge(s_iota, 3)
            dve.tensor_scalar(neg_iota[:, :], iota_i[:, :], -1.0, None, ALU.mult).then_inc(s_iota_f, 1)
            dve.tensor_copy(iota_part[:, :], iota_i[:, :]).then_inc(s_iota_key, 1)
            dve.tensor_copy(iota_key[:, :], iota_key_i).then_inc(s_iota_key, 1)
            dve.wait_ge(s_ident, 2)
            for n in range(PARTS):
                rows = slice(n * D, (n + 1) * D)
                dve.tensor_copy(stack_identity[rows, :], identity[rows, rows]).then_inc(s_stack, 1)
            for c in range(CHUNKS):
                a, b = c * CHUNK, min((c + 1) * CHUNK, SLOTS)
                dve.wait_ge(s_si_mm, min(4 * (c + 1), -(-SLOTS // 4)))
                nm = w_ps[c % 2][:, 0:2, :].rearrange("p a (s d) -> p (a s) d", d=D)
                dve.tensor_tensor(x_nm[:, a:b, :], x_nm[:, a:b, :], nm[:, 0:b - a, :], ALU.add)\
                   .then_inc(s_x1, 1)
            dve.wait_ge(s_group_in, 16)
            dve.tensor_tensor(neg_loc[:, :].rearrange("p (g j t) -> p g j t", j=2, t=TILES),
                              table[:, :, 0:2].unsqueeze(3).broadcast_to([P, PAIRS, 2, TILES]),
                              dst_i[:, :].rearrange("p (g j t) -> p g j t", j=2, t=TILES),
                              ALU.subtract).then_inc(s_tables, 1)
            for k in range(2):
                dve.tensor_scalar(flags[k][:, :, :],
                                  table[0:1, :, FAR_COL + 2 * k:FAR_COL + 2 * k + 2],
                                  float(SLOTS), None, ALU.mult).then_inc(s_flags, 1)
            dve.tensor_scalar(fallback_flags[:, :], table[0:1, :, FAR_COL + 3], float(16 * TILES),
                              None, ALU.mult).then_inc(s_flags, 1)
            dve.wait_ge(s_flags, 3)
            dve.wait_ge(s_eps, 2)
            row = [f[:, :, :].rearrange("p a b -> p (a b)") for f in flags]
            for k in range(2):
                dve.tensor_tensor_scan(far_upto[k][:, :], ones_row[:, :], row[k], 0.0,
                                       ALU.mult, ALU.add).then_inc(s_flags, 1)
            dve.tensor_tensor_scan(fallback_upto[:, :], ones_row[:, 0:PAIRS], fallback_flags[:, :],
                                   0.0, ALU.mult, ALU.add).then_inc(s_flags, 1)
            dve.wait_ge(s_flags, 6)
            for k in range(2):
                dve.tensor_tensor(far_rounds[k][:, :], far_upto[k][:, :], row[k], ALU.subtract)\
                   .then_inc(s_tables, 1)
            dve.tensor_tensor(fallback_rows[:, :], fallback_upto[:, :], fallback_flags[:, :],
                              ALU.subtract).then_inc(s_tables, 1)
            dve.wait_ge(s_tables, 4)
            dve.wait_ge(s_iota_f, 1)
            dve.wait_ge(s_zero, 4)

            def far_windows(k, i, j, group):
                flag = dve.value_load(table[0:1, i, FAR_COL + 2 * k + j:FAR_COL + 2 * k + j + 1],
                                      min_val=0, max_val=1)
                with dve.If(flag):
                    done = dve.value_load(far_rounds[k][0:1, bass.ds(group, 1)], min_val=0,
                                          max_val=GROUPS * SLOTS)
                    if k == 1 and j == 1:
                        nodes = dst_c[:, bass.ds(i * TILES, TILES)]
                        dve.tensor_scalar(far[:, :], key[:, bass.ds(i * TILES, TILES)], -1.0, None,
                                          ALU.is_le).then_inc(s_far_dst[k], 1)
                    else:
                        nodes = dst_i[:, bass.ds(group * TILES, TILES)]
                        dve.tensor_scalar(far[:, :], neg_loc[:, bass.ds(group * TILES, TILES)],
                                          float(-WIN), None, ALU.is_le).then_inc(s_far_dst[k], 1)
                    dve.drain()
                    dve.scalar_tensor_tensor(out=far[:, :], in0=nodes, scalar=1.0,
                                             in1=far[:, :], op0=ALU.add, op1=ALU.mult)
                    dve.drain()
                    dve.tensor_scalar(far[:, :], far[:, :], -1.0, 1.0, ALU.mult, ALU.add)
                    with dve.Fori(0, SLOTS) as w:
                        dve.drain()
                        dve.wait_ge(s_far_win[k], done + w + 1)
                        dve.tensor_tensor(
                            onehot_far[k][:, :, :],
                            neg_iota[:, :].unsqueeze(1).broadcast_to([P, TILES, WIN]),
                            far[:, :].unsqueeze(2).broadcast_to([P, TILES, WIN]),
                            ALU.is_equal).then_inc(s_far_onehot[k], 1)
                        dve.drain()
                        dve.tensor_scalar(far[:, :], far[:, :], float(WIN), None, ALU.add)
                        dve.wait_ge(s_far_win[k], done + w + 2)
                        window = acc[k][:, bass.ds(w * WIN, WIN)]
                        dve.tensor_tensor(window, window, far_ps[k], ALU.add)\
                           .then_inc(s_far_acc[k], 1)
                    dve.wait_ge(s_far_acc[k], done + SLOTS + 1)
                    dve.sem_inc(s_far_done, 1)

            def accumulate(k, i, j, done, group, first):
                if not first:
                    dve.wait_ge(s_acc[k], done)
                far_windows(k, i, j, group)
                base = dve.value_load(table[0:1, i, j:j + 1], min_val=0, max_val=NODES - 1)

                def add():
                    dve.wait_ge(s_win[k], done + 1)
                    window = acc[k][:, bass.ds(base, WIN)]
                    dve.tensor_tensor(window, window, win_ps[rows_of[k], :], ALU.add)\
                       .then_inc(s_acc[k], 1)

                return add

            def messages(g, i, j, first):
                out_m, zz, s = msg[j], z[j], sh_sb[j]
                dve.wait_ge(s_z[0][j], 16 * TILES * (i + 1))
                dve.wait_ge(s_sh[j], 16 * (i + 1))
                if not first:
                    dve.wait_ge(s_zs, 2 * g)
                    dve.wait_ge(s_prod, 2 * g)
                dve.tensor_tensor(
                    v_sh[:, :, :, :].rearrange("p t i m -> p t m i"),
                    zz[:, :, 0:3 * MUL].rearrange("p t (m i) -> p t m i", m=3),
                    s[:, :, 1:4].unsqueeze(3).broadcast_to([P, TILES, 3, MUL]), ALU.mult)\
                   .then_inc(s_vsh, 1)
                dve.tensor_tensor(z_s[:, :, 0:MUL], zz[:, :, 3 * MUL:],
                                  s[:, :, 0:1].broadcast_to([P, TILES, MUL]), ALU.mult)\
                   .then_inc(s_zs, 1)
                dve.wait_ge(s_vsh, g + 1)
                dve.tensor_reduce(z_s[:, :, MUL:], v_sh[:, :, :, :], AX.X, ALU.add).then_inc(s_zs, 1)
                for q in range(2):
                    ts = slice(4 * q, 4 * q + 4)
                    w = w_ps[q]
                    dve.wait_ge(s_w_mm, 2 * g + q + 1)
                    if not first:
                        dve.wait_ge(s_sum_bc, g)
                    dve.tensor_tensor(
                        prod_bc[q][:, :, 3, :, :],
                        w[:, :, 128:192].rearrange("p t (o i) -> p t o i", i=MUL),
                        zz[:, ts, 3 * MUL:].unsqueeze(2).broadcast_to([P, 4, MUL, MUL]), ALU.mult)\
                       .then_inc(s_prod_bc, 1)
                    dve.wait_ge(s_zs, 2 * (g + 1))
                    dve.wait_ge(s_scaled, TILES * (g + 1))
                    dve.tensor_tensor(
                        prod_bc[q][:, :, 0:3, :, :].rearrange("p t m o i -> p m t (o i)"),
                        w[:, :, 192:256].unsqueeze(1).broadcast_to([P, 3, 4, MUL * MUL]),
                        z_v[:, q, :, :, :].rearrange("p m t i -> p (m t) i").unsqueeze(2)
                        .broadcast_to([P, 12, MUL, MUL]), ALU.mult).then_inc(s_prod_bc, 1)
                    if not first:
                        dve.wait_ge(s_sum_a, g)
                    dve.tensor_tensor(
                        prod_a[q][:, :, :, :],
                        w[:, :, 0:128].rearrange("p t (o i) -> p t o i", i=2 * MUL),
                        z_s[:, ts, :].unsqueeze(2).broadcast_to([P, 4, MUL, 2 * MUL]), ALU.mult)\
                       .then_inc(s_prod, 1)
                if not first:
                    dve.wait_ge(s_p_sh, g)
                    dve.wait_ge(s_msg, g)
                if not isinstance(g, int) or g >= 2:
                    dve.wait_ge(s_win[0], g - 1)
                dve.wait_ge(s_prod_bc, 4 * (g + 1))
                dve.tensor_reduce(sums[:, :, :, :].rearrange("p t c o -> p (t c o)"),
                                  products_bc.rearrange("p (n i) -> p n i", i=MUL),
                                  AX.X, ALU.add).then_inc(s_sum_bc, 1)
                dve.wait_ge(s_prod, 2 * (g + 1))
                dve.tensor_reduce(out_m[:, :, 3 * MUL:],
                                  products_a.rearrange("p (t o i) -> p t o i", o=MUL, i=2 * MUL),
                                  AX.X, ALU.add).then_inc(s_sum_a, 1)
                add = None if isinstance(g, int) and g == 0 else \
                    accumulate(0, i if j else i - 1, 1 - j, g - 1, g - 1, isinstance(g, int) and g == 1)
                dve.wait_ge(s_sum_bc, g + 1)
                dve.tensor_tensor(
                    p_sh[:, :, :, :], sums[:, :, 3:4, :].broadcast_to([P, TILES, 3, MUL]),
                    s[:, :, 1:4].unsqueeze(3).broadcast_to([P, TILES, 3, MUL]), ALU.mult)\
                   .then_inc(s_p_sh, 1)
                if add is not None:
                    add()
                dve.wait_ge(s_p_sh, g + 1)
                dve.wait_ge(s_sum_a, g + 1)
                dve.tensor_tensor(
                    out_m[:, :, 0:3 * MUL].rearrange("p t (m o) -> p t m o", m=3),
                    sums[:, :, 0:3, :], p_sh[:, :, :, :], ALU.add).then_inc(s_msg, 1)

            dve.wait_ge(s_source, 1)
            for g in range(4):
                messages(g, g // 2, g % 2, g == 0)
            with dve.Fori(1, PAIRS // 2) as n:
                for m in range(4):
                    messages(4 * n + m, 2 * n + m // 2, m % 2, False)
            accumulate(0, PAIRS - 1, 1, GROUPS - 1, GROUPS - 1, False)()

            def add_chunks(k):
                for c in range(CHUNKS):
                    a, b = c * CHUNK, min((c + 1) * CHUNK, SLOTS)
                    dve.wait_ge(s_nm[k], c + 1)
                    nm = w_ps[c % 2][:, 0:2, :].rearrange("p a (s d) -> p (a s) d", d=D)
                    dve.tensor_tensor(x_nm[:, a:b, :], x_nm[:, a:b, :], nm[:, 0:b - a, :], ALU.add)\
                       .then_inc(s_nm_add[k], 1)

            part = [h_split[:, :, n * D:(n + 1) * D] for n in range(PARTS)]

            def centered(c):
                a, b = c * CHUNK, min((c + 1) * CHUNK, SLOTS)
                dve.wait_ge(s_nm[0], c + 1)
                nm = w_ps[c % 2][:, 0:2, :].rearrange("p a (s d) -> p (a s) d", d=D)
                dve.tensor_tensor(x_nm[:, a:b, :], x_nm[:, a:b, :], nm[:, 0:b - a, :], ALU.add)\
                   .then_inc(s_nm_add[0], 1)
                dve.wait_ge(s_nm_add[0], c + 1)
                dve.tensor_reduce(stat[:, 0, a:b], x_nm[:, a:b, :], AX.X, ALU.add).then_inc(s_ln, 1)
                dve.wait_ge(s_ln, 3 + 2 * c + 1)
                dve.scalar_tensor_tensor(
                    out=h_nm[:, a:b, :], in0=stat[:, 0, a:b].unsqueeze(2).broadcast_to([P, b - a, D]),
                    scalar=-1.0 / D, in1=x_nm[:, a:b, :], op0=ALU.mult, op1=ALU.add).then_inc(s_ln, 1)

            def normed(c):
                a, b = c * CHUNK, min((c + 1) * CHUNK, SLOTS)
                dve.wait_ge(s_sq, 1 + c + 1)
                dve.tensor_reduce(stat[:, 1, a:b], scratch[:, a:b, :], AX.X, ALU.add)\
                   .then_inc(s_var, 1)
                dve.wait_ge(s_std, 1 + c + 1)
                dve.reciprocal(stat[:, 3, a:b], stat[:, 2, a:b]).then_inc(s_inv, 1)
                dve.wait_ge(s_inv, 1 + c + 1)
                dve.scalar_tensor_tensor(
                    out=h_nm[:, a:b, :], in0=h_nm[:, a:b, :], scalar=0.0,
                    in1=stat[:, 3, a:b].unsqueeze(2).broadcast_to([P, b - a, D]),
                    op0=ALU.max, op1=ALU.mult).then_inc(s_h, 1)
                dve.wait_ge(s_h, 1 + c + 1)
                dve.tensor_copy(part[0][:, a:b, :], h_nm[:, a:b, :]).then_inc(s_split, 1)
                dve.wait_ge(s_split, 4 * c + 1)
                dve.tensor_tensor(scratch[:, a:b, :], h_nm[:, a:b, :], part[0][:, a:b, :],
                                  ALU.subtract).then_inc(s_split, 1)
                dve.wait_ge(s_split, 4 * c + 2)
                dve.tensor_copy(part[1][:, a:b, :], scratch[:, a:b, :]).then_inc(s_split, 1)
                dve.wait_ge(s_split, 4 * c + 3)
                dve.tensor_tensor(part[2][:, a:b, :], scratch[:, a:b, :], part[1][:, a:b, :],
                                  ALU.subtract).then_inc(s_split, 1)
                dve.scalar_tensor_tensor(
                    out=x_nm[:, a:b, :], in0=h_nm[:, a:b, :], scalar=one_plus_eps[:, :],
                    in1=x_nm[:, a:b, :], op0=ALU.mult, op1=ALU.add).then_inc(s_x3, 1)

            dve.wait_ge(s_eps, 3)
            dve.tensor_scalar(tile_below[:, :], tile_iota[:, :], float(SPAN), None, ALU.is_lt)
            dve.drain()
            dve.scalar_tensor_tensor(out=tile_mask[:, :], in0=tile_iota[:, :], scalar=0.0,
                                     in1=tile_below[:, :], op0=ALU.is_ge, op1=ALU.mult)
            dve.drain()
            dve.tensor_tensor(tile_node[:, :], tile_iota[:, :], tile_mask[:, :], ALU.mult)
            dve.tensor_tensor(of_tile_sb[:, :, :], table[0:SPREAD, :, LO_COL:LO_COL + CTILES],
                              tile_mask[:, :].unsqueeze(1).broadcast_to([SPREAD, PAIRS, CTILES]), ALU.mult)
            dve.drain()
            dve.tensor_reduce(node_in_tile[:, :], tile_node[:, :], AX.X, ALU.add)
            dve.tensor_reduce(column[:, :], of_tile_sb[:, :, :], AX.X, ALU.add)
            dve.drain()
            dve.scalar_tensor_tensor(out=column[:, :], in0=column[:, :], scalar=node_in_tile[:, :],
                                     in1=table[0:SPREAD, :, 1], op0=ALU.add, op1=ALU.subtract)\
               .then_inc(s_column, 1)
            centered(0)
            for c in range(1, CHUNKS):
                centered(c)
                normed(c - 1)
            normed(CHUNKS - 1)

            def one_hot(i, u, q):
                if q == 0 and not isinstance(i, int):
                    dve.wait_ge(s_win[1], i - 1)
                dve.tensor_tensor(
                    onehot_2[u][:, 2 * q:2 * q + 2, :],
                    neg_iota[:, :].unsqueeze(1).broadcast_to([P, 2, WIN]),
                    neg_loc[:, bass.ds(i * 2 * TILES + 2 * q, 2)].unsqueeze(2).broadcast_to([P, 2, WIN]),
                    ALU.is_equal).then_inc(s_onehot[1], 1)

            def keyed(i, t, r):
                if t >= CTILES:
                    i, t, r = i + 1, t - CTILES, (r + 1) % 4
                tile, b4, column_of = CTILES * i + t, (CTILES * r + t) % KEYED, TILES * i + t
                if not (isinstance(i, int) and tile < KEYED):
                    dve.wait_ge(s_counts_mm, tile - KEYED + 1)
                dve.tensor_scalar(is_part[b4][:, :], iota_part[:, :], src_part[:, bass.ds(column_of, 1)],
                                  None, ALU.is_equal).then_inc(s_keyed, 1)
                dve.tensor_scalar(is_key[b4], iota_key[:, :], key[:, bass.ds(column_of, 1)],
                                  None, ALU.is_equal).then_inc(s_keyed, 1)

            def counts_out(tile, u, t):
                dve.wait_ge(s_counts_mm, tile + 1)
                dve.tensor_copy(
                    counts[u][:, 2 * SLOTS_BANK:, t, :],
                    counts_ps[(u + t) % 2][:, 2, 0:BANK_KEYS].rearrange("p (s n) -> p s n", n=SPAN))\
                   .then_inc(s_counts_dve, 1)

            def place_counted(i, u):
                if not isinstance(i, int) or i >= 4:
                    dve.wait_ge(s_counted_win, i - 3)
                dve.tensor_scalar(place[u][:, :], iota_part[0:SPREAD, :],
                                  column[:, bass.ds(i - 2, 1)], None, ALU.is_equal).then_inc(s_place, 1)
                dve.tensor_scalar(onehot_2[u][:, TILES, :], iota_part[:, :], last_loc[:, bass.ds(i - 2, 1)],
                                  None, ALU.is_equal).then_inc(s_place, 1)

            def add_gathered(i, base):
                dve.wait_ge(s_win[1], i + 1)
                window = acc[1][:, bass.ds(base, WIN)]
                dve.tensor_tensor(window, window, win_ps[rows_of[1], :], ALU.add).then_inc(s_acc[1], 1)

            def add_counted(i, base):
                dve.wait_ge(s_counted_win, i - 1)
                window = acc[1][:, bass.ds(base, WIN)]
                dve.tensor_tensor(window, window, counted_win_ps, ALU.add).then_inc(s_counted_acc, 1)

            def base_of(i, j):
                return dve.value_load(table[0:1, i, j:j + 1], min_val=0, max_val=NODES - 1)

            def second_layer(i, u, r):
                old = not isinstance(i, int) or i >= 2
                for t in range(CTILES):
                    tile = CTILES * i + t
                    keyed(i, t + AHEAD, r)
                    if t < TILES // 2:
                        one_hot(i, u, t)
                    if t == 0 and old:
                        place_counted(i, u)
                    if t == WINDOWS_AT + 1:
                        with dve.If(flag):
                            if not isinstance(i, int) or i >= 3:
                                dve.wait_ge(s_counted_acc, i - 2)
                            if not isinstance(i, int) or i >= 1:
                                dve.wait_ge(s_acc[1], i)
                            far_windows(1, i, 0, 2 * i)
                            far_windows(1, i, 1, 2 * i + 1)
                    if t == ADD_AT:
                        if not isinstance(i, int) or i >= 3:
                            dve.wait_ge(s_counted_acc, i - 2)
                        if old:
                            dve.wait_ge(s_counted_win, i - 1)
                        add_gathered(i, gathered_base)
                        if old:
                            dve.wait_ge(s_acc[1], i + 1)
                            add_counted(i, counted_base)
                    if t - 1 in OUT_DVE:
                        if old and t - 1 == OUT_DVE[0]:
                            dve.wait_ge(s_counted, i - 1)
                        counts_out(tile - 1, u, t - 1)
                    if t == 0:
                        flag = dve.value_load(table[0:1, i, ANY_COL:ANY_COL + 1], min_val=0, max_val=1)
                    if t == 3:
                        gathered_base = base_of(i, 0)
                    if t == 4 and old:
                        counted_base = base_of(i - 2, 1)

            dve.wait_ge(s_keys, 2)
            dve.wait_ge(s_column, 1)
            dve.wait_ge(s_rezero, 1)
            dve.wait_ge(s_x3, CHUNKS)
            for t in range(AHEAD):
                keyed(0, t, 0)
            second_layer(0, 0, 0)
            dve.wait_ge(s_w_mm, 2 * GROUPS)
            dve.wait_ge(s_onehot[0], GROUPS)
            for i in range(1, 6):
                second_layer(i, i % 2, i % 4)
            with dve.Fori(1, (PAIRS - 2) // 4) as m:
                for k in range(2, 6):
                    second_layer(4 * m + k, k % 2, k % 4)
            for i in (PAIRS, PAIRS + 1):
                place_counted(i, i % 2)
            for i in (PAIRS, PAIRS + 1):
                dve.wait_ge(s_counted_acc, i - 2)
                add_counted(i, base_of(i - 2, 1))
            add_chunks(1)


FEATURES = np.concatenate([MUL + np.arange(3 * MUL).reshape(MUL, 3).T.ravel(), np.arange(MUL)])


def weight_order():
    cols = np.arange(W_NUMEL).reshape(4, MUL, MUL)
    w_000, w_011, w_101, w_110 = (c.T for c in cols)
    return np.concatenate([np.concatenate([w_000, w_110], axis=1).ravel(), w_011.ravel(), w_101.ravel()])


def kernel(x, src, dst, edge_attr_32, edge_attr_4, L0_gnn_W1, L0_gnn_b1, L0_gnn_W2, L0_gnn_b2,
           L0_gnn_si_w0, L0_gnn_si_w1, L1_gnn_eps):
    import concourse.bacc as bacc
    from concourse.bass_utils import run_bass_kernel_spmd

    def padded(a, n, value=0):
        a = np.asarray(a)
        out = np.full((n,) + a.shape[1:], value, a.dtype)
        out[:a.shape[0]] = a
        return out

    order = weight_order()
    src_p, dst_p = padded(src, EDGES), padded(dst, EDGES, N_NODES)

    def counted(a):
        return a.reshape(PAIRS, 2, TILES, P)[:, 1].transpose(2, 0, 1).reshape(P, PAIRS * TILES)

    arrays = {
        "x": padded(x, NODES)[:, FEATURES].reshape(P, SLOTS, D),
        "src": src_p.reshape(GROUPS, P, TILES),
        "src_last": src_p.reshape(PAIRS, 2, TILES, P, 1)[:, 1, CTILES],
        "src_counted": counted(src_p),
        "dst_counted": counted(dst_p),
        "dst_groups": dst_p.reshape(PAIRS, 2, GROUP),
        "dst_tiles": dst_p.reshape(GROUPS, P, TILES).transpose(1, 0, 2).reshape(P, GROUPS * TILES),
        "edge_t": padded(edge_attr_32, EDGES).reshape(GROUPS, P, SUBS, TILES // SUBS, D_EDGE)
        .transpose(0, 2, 4, 3, 1).reshape(GROUPS, P, SUB),
        "sh": padded(edge_attr_4, EDGES).reshape(GROUPS, P, TILES, 4),
        "w1": np.asarray(L0_gnn_W1),
        "b1": np.asarray(L0_gnn_b1).reshape(D_MLP, 1),
        "w2": np.asarray(L0_gnn_W2)[:, order],
        "b2": np.asarray(L0_gnn_b2)[order].reshape(1, W_NUMEL),
        "si0": np.asarray(L0_gnn_si_w0),
        "si1": np.asarray(L0_gnn_si_w1),
        "eps": np.asarray(L1_gnn_eps).reshape(1, 1),
    }
    nc = bacc.Bacc("TRN2", target_bir_lowering=False, num_devices=1)
    args, ins = [], {}
    for name, a in arrays.items():
        a = np.ascontiguousarray(a)
        ins[f"in_{name}"] = a
        args.append(nc.dram_tensor(f"in_{name}", a.shape, mybir.dt.from_np(a.dtype),
                                   kind="ExternalInput").ap())
    args.append(nc.dram_tensor("out_nodes", (P, SLOTS, D), F32, kind="ExternalOutput").ap())
    build(nc, *args)
    r = run_bass_kernel_spmd(nc, [ins], core_ids=[0])
    got = r.results[0]["out_nodes"].reshape(NODES, D)[:N_NODES]
    back = np.empty(D, np.int64)
    back[FEATURES] = np.arange(D)
    return np.ascontiguousarray(got[:, back])
```
